# Optimizing a Trainium2 kernel written in Bass

```python
import numpy as np
import jax
import jax.numpy as jnp

def _softmax(x, axis=-1):
    return jax.nn.softmax(x, axis=axis)

def _gelu(x):
    return jax.nn.gelu(x, approximate=True)

def _silu(x):
    return jax.nn.silu(x)

def _sigmoid(x):
    return jax.nn.sigmoid(x)

def _layernorm(x, axis=-1, eps=1e-05):
    m = jnp.mean(x, axis=axis, keepdims=True)
    v = jnp.var(x, axis=axis, keepdims=True)
    return (x - m) / jnp.sqrt(v + eps)

def _scatter_add(tgt, idx, src, axis=0):
    return tgt.at[idx].add(src)

def _segment_sum(src, seg, n):
    return jax.ops.segment_sum(src, seg, n)
kernel_name = 'mk_pixart_resid_d1_seqx_r4_12a65c'

def setup_inputs(seed: int=0):
    np.random.seed(seed)
    _w = jnp.asarray

    def _rec_inputs():
        import jax
        import jax.numpy as jnp
        _rk = jax.random.key(seed)
        x = -0.0002928 + 1 * jax.random.normal(jax.random.fold_in(_rk, 1), (16, 256, 512), jnp.float32)
        _lenS = 256 - jax.random.randint(jax.random.fold_in(_rk, 7), (16,), 0, max(1, 256 // 4) + 1, jnp.int32)
        _lenS2 = 256 - jax.random.randint(jax.random.fold_in(_rk, 8), (16,), 0, max(1, 256 // 4) + 1, jnp.int32)
        _ctx_2048P = jax.random.normal(jax.random.fold_in(_rk, 11), (16, 16, 512), jnp.float32)
        _ctx_2048c = jax.random.dirichlet(jax.random.fold_in(_rk, 511), 0.3 * jnp.ones((16,), jnp.float32), (16, 256))
        _ctx_2048t = jnp.einsum('bsk,bkd->bsd', _ctx_2048c, _ctx_2048P)
        _ctx_2048t = _ctx_2048t * jax.lax.rsqrt(jnp.mean(jnp.square(_ctx_2048t)) + 1e-12) * 0.953939
        ctx_2048 = -1.39393e-06 + 0.999914 * (_ctx_2048t + 0.3 * jax.random.normal(jax.random.fold_in(_rk, 611), (16, 256, 512), jnp.float32))
        itok_B_779_1933 = jax.random.randint(jax.random.fold_in(_rk, 12), (16,), 779, 1934, jnp.int32)
        return (x, ctx_2048, itok_B_779_1933)
    x, ctx_2048, itok_B_779_1933 = _rec_inputs()

    def _L0_xcond_setup():
        import jax, jax.numpy as jnp
        import numpy as np
        NUM_HEADS = 8
        HEAD_DIM = 64
        AVG_K_LENGTH = 20
        SCALE = 1.0 / (HEAD_DIM ** 0.5 * float(np.log(AVG_K_LENGTH)))
        key = jax.random.key(seed)
        k1, k2, k3, k4 = jax.random.split(key, 4)
        B, HD, LQ, LK = (4, NUM_HEADS * HEAD_DIM, 512, 512)
        q = jax.random.normal(k1, (B, HD, LQ), dtype=jnp.float32)
        k = jax.random.normal(k2, (B, HD, LK), dtype=jnp.float32)
        v = jax.random.normal(k3, (B, HD, LK), dtype=jnp.float32)
        k_length = jax.random.randint(k4, (B,), 128, LK + 1, dtype=jnp.int32)
        return {'q': q, 'k': k, 'v': v, 'k_length': k_length}
    _L0_xcond_all = _L0_xcond_setup()
    _L0_xcond_in = {k: v for k, v in _L0_xcond_all.items() if k in ()}
    del _L0_xcond_all

    def _L0_ffn_setup():
        import jax, jax.numpy as jnp
        import numpy as np
        import math
        D_MODEL = 512
        D_FF = 2048
        NUM_EXPERTS = 8
        TOP_K = 2
        CAPACITY_FACTOR = 1.25
        BATCH, SEQ = (4, 512)

        def _moe_forward(x, Wg, w1, w2):
            B, T, d = x.shape
            S = B * T
            E, K = (NUM_EXPERTS, TOP_K)
            C = math.ceil(CAPACITY_FACTOR * S * K / E)
            xr = x.reshape(S, d)
            probs = jax.nn.softmax(xr @ Wg, axis=-1)
            gate_vals, expert_idx = jax.lax.top_k(probs, K)
            flat_e = expert_idx.reshape(-1)
            oh = jax.nn.one_hot(flat_e, E, dtype=jnp.int32)
            pos = jnp.sum((jnp.cumsum(oh, axis=0) - 1) * oh, axis=1)
            kept = pos < C
            i = jnp.arange(S * K)
            slot = i % K * S + i // K
            sentinel = S * K
            pos_w = jnp.where(kept, pos, C)
            dispatch_mask = jnp.full((E, C), sentinel, dtype=jnp.int32)
            dispatch_mask = dispatch_mask.at[flat_e, pos_w].set(slot.astype(jnp.int32), mode='drop')
            combine_weights = (gate_vals * kept.reshape(S, K)).T
            dispatched = xr[dispatch_mask.reshape(-1) % S].reshape(E, C, d)
            h = jax.nn.relu(jnp.einsum('ecd,edf->ecf', dispatched, w1))
            expert_out = jnp.einsum('ecf,efd->ecd', h, w2)
            rerouted = jnp.zeros((S * K + 1, d), dtype=expert_out.dtype)
            rerouted = rerouted.at[dispatch_mask.reshape(-1)].set(expert_out.reshape(-1, d))
            rerouted = rerouted[:-1].reshape(K, S, d)
            out = jnp.einsum('ks,ksm->sm', combine_weights, rerouted)
            return out.reshape(B, T, d)
        key = jax.random.key(seed)
        k1, k2, k3, k4 = jax.random.split(key, 4)
        x = jax.random.normal(k1, (BATCH, SEQ, D_MODEL), dtype=jnp.float32)
        Wg = jax.random.normal(k2, (D_MODEL, NUM_EXPERTS), dtype=jnp.float32) * 0.02
        w1 = jax.random.normal(k3, (NUM_EXPERTS, D_MODEL, D_FF), dtype=jnp.float32) * 0.02
        w2 = jax.random.normal(k4, (NUM_EXPERTS, D_FF, D_MODEL), dtype=jnp.float32) * 0.02
        return {'x': x, 'Wg': Wg, 'w1': w1, 'w2': w2}
    _L0_ffn_all = _L0_ffn_setup()
    _L0_ffn_in = {k: v for k, v in _L0_ffn_all.items() if k in ('Wg', 'w1', 'w2')}
    del _L0_ffn_all
    return {'x': x, 'ctx_2048': ctx_2048, 'itok_B_779_1933': itok_B_779_1933, 'L0_ffn_Wg': _L0_ffn_in['Wg'], 'L0_ffn_w1': _L0_ffn_in['w1'], 'L0_ffn_w2': _L0_ffn_in['w2']}

def reference(x, ctx_2048, itok_B_779_1933, L0_ffn_Wg, L0_ffn_w1, L0_ffn_w2):
    import jax
    import jax.numpy as jnp

    def _L0_xcond_ref(q, k, v, k_length):
        import jax, jax.numpy as jnp
        import numpy as np
        NUM_HEADS = 8
        HEAD_DIM = 64
        AVG_K_LENGTH = 20
        SCALE = 1.0 / (HEAD_DIM ** 0.5 * float(np.log(AVG_K_LENGTH)))
        b, hd, lq = q.shape
        lk = k.shape[-1]
        d = hd // NUM_HEADS
        qh = q.reshape(b, NUM_HEADS, d, lq)
        kh = k.reshape(b, NUM_HEADS, d, lk)
        vh = v.reshape(b, NUM_HEADS, d, lk)
        s = SCALE * jnp.log(k_length.astype(jnp.float32))[:, None, None, None]
        attn = jnp.einsum('bhdq,bhdk->bhqk', qh, kh)
        attn = jax.nn.softmax(s * attn, axis=-1)
        out = jnp.einsum('bhqk,bhdk->bhdq', attn, vh)
        return out.reshape(b, hd, lq)

    def _L0_ffn_ref(x, Wg, w1, w2):
        import jax, jax.numpy as jnp
        import numpy as np
        import math
        D_MODEL = 512
        D_FF = 2048
        NUM_EXPERTS = 8
        TOP_K = 2
        CAPACITY_FACTOR = 1.25
        BATCH, SEQ = (4, 512)

        def _moe_forward(x, Wg, w1, w2):
            B, T, d = x.shape
            S = B * T
            E, K = (NUM_EXPERTS, TOP_K)
            C = math.ceil(CAPACITY_FACTOR * S * K / E)
            xr = x.reshape(S, d)
            probs = jax.nn.softmax(xr @ Wg, axis=-1)
            gate_vals, expert_idx = jax.lax.top_k(probs, K)
            flat_e = expert_idx.reshape(-1)
            oh = jax.nn.one_hot(flat_e, E, dtype=jnp.int32)
            pos = jnp.sum((jnp.cumsum(oh, axis=0) - 1) * oh, axis=1)
            kept = pos < C
            i = jnp.arange(S * K)
            slot = i % K * S + i // K
            sentinel = S * K
            pos_w = jnp.where(kept, pos, C)
            dispatch_mask = jnp.full((E, C), sentinel, dtype=jnp.int32)
            dispatch_mask = dispatch_mask.at[flat_e, pos_w].set(slot.astype(jnp.int32), mode='drop')
            combine_weights = (gate_vals * kept.reshape(S, K)).T
            dispatched = xr[dispatch_mask.reshape(-1) % S].reshape(E, C, d)
            h = jax.nn.relu(jnp.einsum('ecd,edf->ecf', dispatched, w1))
            expert_out = jnp.einsum('ecf,efd->ecd', h, w2)
            rerouted = jnp.zeros((S * K + 1, d), dtype=expert_out.dtype)
            rerouted = rerouted.at[dispatch_mask.reshape(-1)].set(expert_out.reshape(-1, d))
            rerouted = rerouted[:-1].reshape(K, S, d)
            out = jnp.einsum('ks,ksm->sm', combine_weights, rerouted)
            return out.reshape(B, T, d)
        return _moe_forward(x, Wg, w1, w2)
    x = x + _L0_xcond_ref(_layernorm(x, axis=-1), ctx_2048, ctx_2048, itok_B_779_1933)
    x = x + _L0_ffn_ref(_layernorm(x, axis=-1), L0_ffn_Wg, L0_ffn_w1, L0_ffn_w2)
    return x

_drawn_inputs = setup_inputs


def setup_inputs(seed=0):
    import zlib

    import numpy as np

    out = dict(_drawn_inputs(seed))
    spreads = {}
    factors = {}
    for name, (base, spread) in spreads.items():
        noise = np.random.default_rng([zlib.crc32(name.encode()), seed]).standard_normal(out[name].shape)
        drawn = base * np.exp(spread * noise) if base else spread * noise
        out[name] = jnp.asarray(drawn.astype(out[name].dtype))
    for name, factor in factors.items():
        out[name] = (out[name] * factor).astype(out[name].dtype)
    return out
```

```python
from contextlib import ExitStack

import concourse.bass as bass
import numpy as np
from concourse import mybir

F32 = mybir.dt.float32
F32R = mybir.dt.float32r
I32 = mybir.dt.int32
U32 = mybir.dt.uint32
ALU = mybir.AluOpType
ACT = mybir.ActivationFunctionType
AX = mybir.AxisListType.X

P = 128
B, CH, D = 16, 256, 512
HEADS = 8
HD = CH // HEADS
HPG = P // HD
G = B * CH // P
S = B * CH
NC4 = D // P
E, TOPK, FF = 8, 2, 2048
CAP = -(-5 * S * TOPK // (4 * E))
T = 256
TILES = CAP // T
NF = FF // P
ROW = 528
GATE0, IDCOL = D, D + E
EPS = 1e-5
SCALE = 1.0 / (64 ** 0.5 * float(np.log(20)))
U = 8
STACK = 3 * HD
MROWS = 2 * HPG
PIECES = 16
NRAW = 4

PREP, LOADX = -2, -3
ST, PV, OUT, LN = 2, 3, 4, 5


class Slot:

    def __init__(self, it, k):
        self.it, self.k = it, k

    def has(self, lag):
        if not isinstance(self.it, int):
            return True
        return 0 <= U * self.it + self.k - lag < G

    def group(self, lag):
        return self.it * U + (self.k - lag)

    def rounds(self, lag, ring):
        g = self.k - lag
        return self.it * (U // ring) + (g // ring + 1)

    def ring(self, lag, ring):
        return (self.k - lag) % ring

    def wait(self, eng, sem, lag, each=1, minus=0, ahead=False):
        if not isinstance(self.it, int):
            eng.wait_ge(sem, self.it * (U * each) + ((self.k - lag + 1) * each - minus))
            return
        g = min(U * self.it + self.k - lag, G - 1)
        if (g + 1) * each - minus > 0:
            eng.wait_ge(sem, (g + 1) * each - minus)


def slots(eng):
    for k in range(LOADX, U):
        yield Slot(k // U, k % U)
    with eng.Fori(1, G // U - 1) as it:
        for k in range(U):
            yield Slot(it, k)
    for k in range(G - U, G + U + 2):
        yield Slot(k // U, k % U)


def layer(nc, x, ctx, klen, wg, w1, w2, out, disp):
    x_rows = x.rearrange("b c l -> (b c) l")
    ctx_rows = ctx.rearrange("b c l -> (b c) l")
    out_rows = out.rearrange("b c l -> (b c) l")
    with nc.sbuf_tensor("totals", [P, E], I32) as totals:
        attention_and_dispatch(nc, x_rows, ctx_rows, klen, wg, out_rows, disp, totals)
        experts(nc, w1, w2, out_rows, disp, totals)


def attention_and_dispatch(nc, x_rows, ctx_rows, klen, wg, out_rows, disp, totals):
    with ExitStack() as stack:
        def sb(name, shape, dt=F32):
            return stack.enter_context(nc.sbuf_tensor(name, shape, dt))

        def sem(name):
            return stack.enter_context(nc.semaphore(name))

        def sems(name, n):
            return [sem(f"{name}{i}") for i in range(n)]

        ident = sb("ident", [P, P])
        ones = sb("ones", [P, P])
        earlier = sb("earlier", [P, P])
        wg_sb = sb("wg_sb", [P, NC4, E])
        klen_i = sb("klen_i", [P, B], I32)
        klen_f = sb("klen_f", [P, B])
        sharp = sb("sharp", [P, B])
        nhalf = sb("nhalf", [P, 1])
        tok_i = sb("tok_i", [P, G], I32)
        tok = sb("tok", [P, G])
        e_i = sb("e_i", [P, E], I32)
        e_f = sb("e_f", [P, E])
        e_row0 = sb("e_row0", [P, E])
        counted = sb("counted", [P, E])

        xt = [sb(f"xt{i}", [P, D]) for i in range(8)]
        ct = [sb(f"ct{i}", [P, D]) for i in range(4)]
        qst = [sb(f"qst{i}", [P, HPG, D], F32R) for i in range(4)]
        kst = [sb(f"kst{i}", [P, HPG, D], F32R) for i in range(4)]
        probs = [sb(f"probs{i}", [P, HPG, NC4, D]) for i in range(2)]
        sel = probs[0][:, 0]
        vt = [sb(f"vt{i}", [P, NC4, P]) for i in range(4)]
        qf = sb("qf", [P, D])
        qhi = [sb(f"qhi{i}", [P, D], F32R) for i in range(2)]
        qlo = [sb(f"qlo{i}", [P, D], F32R) for i in range(2)]
        khi = [sb(f"khi{i}", [P, D], F32R) for i in range(2)]
        klo = [sb(f"klo{i}", [P, D], F32R) for i in range(2)]
        st1 = [sb(f"st1_{i}", [P, 12]) for i in range(2)]
        nmax = [sb(f"nmax{i}", [P, NC4, HPG]) for i in range(2)]
        nmax_hl = [sb(f"nmax_hl{i}", [P, NC4, HD]) for i in range(2)]
        mrow = sb("mrow", [HD, D], F32R)
        o_sb = sb("o_sb", [P, D])
        l_sb = sb("l_sb", [P, D])
        linv = [sb(f"linv{i}", [P, NC4, HPG]) for i in range(2)]
        x1 = [sb(f"x1_{i}", [P, D]) for i in range(2)]
        st2 = [sb(f"st2_{i}", [P, 12]) for i in range(2)]
        xrow = [sb(f"xrow{i}", [P, ROW]) for i in range(8)]
        x2t = sb("x2t", [P, D])
        fill = xrow[7]
        lg = [sb(f"lg{i}", [P, 2, E]) for i in range(2)]
        lmax = sb("lmax", [P, 2])
        lsub = sb("lsub", [P, 2, E])
        lexp = sb("lexp", [P, 2, E])
        zsum = sb("zsum", [P, 2])
        zinv = sb("zinv", [P, 2])
        pr = sb("pr", [P, 2, E])
        top = sb("top", [P, 2, 8])
        topi = sb("topi", [P, 2, 8], U32)
        topf = sb("topf", [P, 2, TOPK])
        hot = sb("hot", [P, 2, TOPK, E])
        picked = sb("picked", [P, 2, E])
        before = sb("before", [P, 2, E])
        over = sb("over", [P, 2, E])
        place = sb("place", [P, 2, E])
        chosen = sb("chosen", [P, 2, TOPK, E])
        rowf = sb("rowf", [P, 2, TOPK])
        rowd = [sb(f"rowd{i}", [P, 2 * TOPK], I32) for i in range(2)]
        zeros = sb("zeros", [P, 2 * TOPK], I32)
        rowi = [sb(f"rowi{i}", [P, 2 * TOPK], I32) for i in range(2)]

        ps_s = [stack.enter_context(nc.psum_tensor(f"ps_s{i}", [P, D], F32)) for i in range(2)]
        ps_t = [stack.enter_context(nc.psum_tensor(f"ps_t{i}", [P, D], F32)) for i in range(2)]
        ps_o = stack.enter_context(nc.psum_tensor("ps_o", [P, D], F32))
        ps_l = stack.enter_context(nc.psum_tensor("ps_l", [P, D], F32))
        ps_a = stack.enter_context(nc.psum_tensor("ps_a", [P, D], F32))
        ps_b = stack.enter_context(nc.psum_tensor("ps_b", [P, D], F32))

        const_ld = sem("const_ld")
        zeroed = sem("zeroed")
        pool_const = sem("pool_const")
        dve_const = sem("dve_const")
        sharp_ln = sem("sharp_ln")
        sel_ready = sem("sel_ready")
        fill_st = sem("fill_st")
        x_ld = sems("x_ld", 8)
        c_ld = sems("c_ld", 4)
        stack_ld = sems("stack_ld", 4)
        mrow_ld = sems("mrow_ld", 4)
        x1_st = sems("x1_st", 2)
        row_st = sems("row_st", 8)
        stat1 = sem("stat1"); var1 = sem("var1"); veps1 = sem("veps1"); rstd1 = sem("rstd1")
        rs1 = sem("rs1"); q_ready = sem("q_ready")
        qhi_ready = sem("qhi_ready"); khi_ready = sem("khi_ready")
        qlo_ready = sem("qlo_ready"); klo_ready = sem("klo_ready")
        s_done = sem("s_done")
        max_done = sem("max_done")
        nmax_hi = sem("nmax_hi"); nmax_ready = sem("nmax_ready")
        m_done = sem("m_done"); mrow_ready = sem("mrow_ready")
        st_done = sem("st_done")
        exp_done = sem("exp_done")
        vt_done = sem("vt_done"); vt_ready = sem("vt_ready")
        pv_done = sem("pv_done"); o_saved = sem("o_saved"); l_saved = sem("l_saved")
        lt_done = sem("lt_done"); linv_ready = sem("linv_ready")
        r_done = sem("r_done"); scaled = sem("scaled"); x1_ready = sem("x1_ready")
        stat2 = sem("stat2"); var2 = sem("var2"); veps2 = sem("veps2"); rstd2 = sem("rstd2")
        x2_ready = sem("x2_ready"); zeros_ready = sem("zeros_ready")
        x2t_done = sem("x2t_done"); x2t_ready = sem("x2t_ready")
        lg_done = sem("lg_done"); lg_saved = sem("lg_saved")
        total_done = sem("total_done"); total_ready = sem("total_ready")
        rt = {n: sem("rt_" + n) for n in (
            "lmax", "lsub", "lexp", "zsum", "zinv", "pr", "top", "topi", "topf", "hot", "picked", "first",
            "before", "counted", "pos", "place0", "over", "place", "chosen", "rowf", "rowd", "rowi", "gate")}

        block = stack.enter_context(nc.Block())

        @block.sync
        def _(sp):
            sp.dma_start(wg_sb[:], wg.rearrange("(c p) e -> p c e", p=P)).then_inc(const_ld, 16)
            sp.dma_start(klen_i[:], klen.rearrange("(a b) -> a b", a=1).to_broadcast([P, B])).then_inc(const_ld, 16)
            for s in slots(sp):
                if s.has(1):
                    s.wait(sp, mrow_ready, 1)
                    sp.dma_start(qst[s.ring(1, 4)][STACK:STACK + MROWS, :, :].bitcast(F32),
                                 mrow[0:MROWS, :].bitcast(F32).unsqueeze(1).to_broadcast([MROWS, HPG, D])
                                 ).then_inc(mrow_ld[s.ring(1, 4)], 16)
                if s.has(LOADX):
                    s.wait(sp, x1_ready, LOADX + 8)
                    sp.dma_start(xt[s.ring(LOADX, 8)][:], x_rows[bass.ds(s.group(LOADX) * P, P), :]
                                 ).then_inc(x_ld[s.ring(LOADX, 8)], 16)
                    s.wait(sp, vt_done, LOADX + 4)
                    s.wait(sp, klo_ready, LOADX + 4)
                    sp.dma_start(ct[s.ring(LOADX, 4)][:], ctx_rows[bass.ds(s.group(LOADX) * P, P), :]
                                 ).then_inc(c_ld[s.ring(LOADX, 4)], 16)
                if s.has(OUT + 1):
                    s.wait(sp, x1_ready, OUT + 1)
                    sp.dma_start(out_rows[bass.ds(s.group(OUT + 1) * P, P), :], x1[s.ring(OUT + 1, 2)][:]
                                 ).then_inc(x1_st[s.ring(OUT + 1, 2)], 16)
                if s.has(PREP):
                    s.wait(sp, st_done, PREP + 4, each=16)
                    s.wait(sp, qhi_ready, PREP)
                    s.wait(sp, khi_ready, PREP)
                    s.wait(sp, qlo_ready, PREP)
                    s.wait(sp, klo_ready, PREP)
                    i, j2 = s.ring(PREP, 4), s.ring(PREP, 2)
                    for h in range(HPG):
                        rows = slice(HD * h, HD * h + HD)
                        for n, (q, k) in enumerate(((qhi, khi), (qhi, klo), (qlo, khi))):
                            to = slice(HD * n, HD * n + HD)
                            sp.dma_start(qst[i][to, h, :].bitcast(F32), q[j2][rows, :].bitcast(F32)).then_inc(stack_ld[i], 16)
                            sp.dma_start(kst[i][to, h, :].bitcast(F32), k[j2][rows, :].bitcast(F32)).then_inc(stack_ld[i], 16)
            for n in range(2):
                sp.wait_ge(x1_st[n], 16 * (G // 2))

        @block.gpsimd
        def _(pool):
            nc.gpsimd.memset(ident[:], 0.0).then_inc(zeroed, 1)
            nc.gpsimd.memset(ones[:], 1.0).then_inc(zeroed, 1)
            nc.gpsimd.memset(nhalf[:], -0.5).then_inc(pool_const, 1)
            nc.gpsimd.memset(zeros[:], 0).then_inc(zeros_ready, 1)
            pool.wait_ge(zeros_ready, 1)
            nc.gpsimd.iota(tok_i[:], [[P, G]], base=0, channel_multiplier=1).then_inc(pool_const, 1)
            nc.gpsimd.iota(e_i[:], [[1, E]], base=0, channel_multiplier=0).then_inc(pool_const, 1)
            pool.wait_ge(zeroed, 2)
            nc.gpsimd.affine_select(out=ident[:], in_=ident[:], compare_op=ALU.not_equal, fill=1.0, base=0,
                                    pattern=[[-1, P]], channel_multiplier=1).then_inc(pool_const, 1)
            nc.gpsimd.affine_select(out=earlier[:], in_=ones[:], compare_op=ALU.is_gt, fill=0.0, base=0,
                                    pattern=[[1, P]], channel_multiplier=-1).then_inc(pool_const, 1)
            pool.wait_ge(pool_const, 5)
            pool.wait_ge(dve_const, 1)
            for part in range(2):
                if part:
                    pool.wait_ge(zeroed, 3)
                nc.gpsimd.affine_select(out=sel[STACK:P], in_=sel[STACK:P], compare_op=ALU.not_equal, fill=1.0,
                                        base=-HPG * part, pattern=[[-1, HPG], [0, D]],
                                        channel_multiplier=1).then_inc(zeroed, 1)
            for s in slots(pool):
                if s.has(PREP):
                    i = s.ring(PREP, 2)
                    s.wait(pool, veps1, PREP)
                    nc.gpsimd.tensor_tensor(st1[i][:, 9:10], st1[i][:, 8:9], nhalf[:], ALU.pow).then_inc(rstd1, 1)
                    if s.has(PREP + 2):
                        pool.wait_ge(stack_ld[s.ring(PREP + 2, 4)], s.rounds(PREP + 2, 4) * (16 * 24))
                    s.wait(pool, khi_ready, PREP)
                    nc.gpsimd.tensor_tensor(klo[i][:], ct[s.ring(PREP, 4)][:], khi[i][:].bitcast(F32),
                                            ALU.subtract).then_inc(klo_ready, 1)
                    s.wait(pool, qhi_ready, PREP)
                    nc.gpsimd.tensor_tensor(qlo[i][:], qf[:], qhi[i][:].bitcast(F32),
                                            ALU.subtract).then_inc(qlo_ready, 1)
                i9 = s.ring(9, 4) // 2
                b9 = s.it * (U // 2) + ((s.k - 9) // 2 + 1)
                if s.k % 2 and s.has(9):
                    pool.wait_ge(rt["rowd"], b9)
                    pool.wait_ge(rt["gate"], b9)
                    nc.gpsimd.tensor_tensor(rowi[i9][:], rowd[i9][:], zeros[:], ALU.add
                                            ).then_inc(rt["rowi"], 1)
                    pool.wait_ge(rt["rowi"], b9)
                if s.has(OUT):
                    s.wait(pool, veps2, OUT)
                    i = s.ring(OUT, 2)
                    nc.gpsimd.tensor_tensor(st2[i][:, 9:10], st2[i][:, 8:9], nhalf[:], ALU.pow).then_inc(rstd2, 1)
                if s.k % 2 and s.has(9):
                    pool.wait_ge(fill_st, 16 * E)
                    for half in range(2):
                        for k in range(TOPK):
                            r = s.ring(9 - half, 8)
                            nc.gpsimd.indirect_dma_start(
                                out=disp[:, :], in_=xrow[r][:], in_offset=None,
                                out_offset=bass.IndirectOffsetOnAxis(
                                    ap=rowi[i9][:, TOPK * half + k:TOPK * half + k + 1].bitcast(U32), axis=0),
                                bounds_check=E * CAP - 1, oob_is_err=False).then_inc(row_st[r], 16)
                    for half in range(2):
                        pool.wait_ge(row_st[s.ring(9 - half, 8)], s.rounds(9 - half, 8) * (16 * TOPK))

        @block.scalar
        def _(act):
            act.wait_ge(const_ld, 32)
            act.wait_ge(dve_const, 4)
            nc.scalar.activation(sharp[:], klen_f[:], ACT.Ln).then_inc(sharp_ln, 1)
            rows = disp.rearrange("(e n p) w -> e p n w", e=E, p=P)
            for e in range(E):
                act.dma_start(rows[e], fill[:].unsqueeze(1).to_broadcast([P, CAP // P, ROW])).then_inc(fill_st, 16)
            for s in slots(act):
                for j in range(HPG):
                    if j == 0 and s.has(OUT):
                        s.wait(act, pv_done, OUT)
                        s.wait(act, lt_done, OUT + 1)
                        nc.scalar.activation(l_sb[:], ps_l[:], ACT.Copy).then_inc(l_saved, 1)
                        s.wait(act, x1_ready, OUT + 1)
                        nc.scalar.activation(o_sb[:], ps_o[:], ACT.Copy).then_inc(o_saved, 1)
                    if s.has(ST):
                        for c in range(NC4):
                            s.wait(act, st_done, ST, each=16, minus=15 - (4 * j + c))
                            if j == 0 and c == 0:
                                s.wait(act, pv_done, ST + 2)
                            nc.scalar.activation(probs[s.ring(ST, 2)][:, j, c, :], ps_t[c % 2][:], ACT.Exp
                                                 ).then_inc(exp_done, 1)
                    if j == 1 and s.has(0):
                        s.wait(act, vt_done, 0)
                        s.wait(act, pv_done, 4)
                        nc.scalar.activation(vt[s.ring(0, 4)][:].rearrange("p c n -> p (c n)"), ps_a[:], ACT.Copy
                                             ).then_inc(vt_ready, 1)
                    if j == 1 and s.has(LN):
                        s.wait(act, x2t_done, LN)
                        s.wait(act, lg_done, LN + 1)
                        nc.scalar.activation(x2t[:], ps_b[:], ACT.Copy).then_inc(x2t_ready, 1)
                    if j == 2 and s.has(PREP):
                        if s.has(PREP + 2):
                            act.wait_ge(stack_ld[s.ring(PREP + 2, 4)], s.rounds(PREP + 2, 4) * (16 * 24))
                        act.wait_ge(c_ld[s.ring(PREP, 4)], s.rounds(PREP, 4) * 16)
                        nc.scalar.activation(khi[s.ring(PREP, 2)][:], ct[s.ring(PREP, 4)][:], ACT.Copy
                                             ).then_inc(khi_ready, 1)
                        s.wait(act, q_ready, PREP)
                        nc.scalar.activation(qhi[s.ring(PREP, 2)][:], qf[:], ACT.Copy
                                             ).then_inc(qhi_ready, 1)
                    if j == 3 and s.k % 2 and s.has(7):
                        act.wait_ge(rt["lsub"], s.it * (U // 2) + ((s.k - 7) // 2 + 1))
                        nc.scalar.activation(lexp[:], lsub[:], ACT.Exp).then_inc(rt["lexp"], 1)
            act.wait_ge(fill_st, 16 * E)

        @block.vector
        def _(dve):
            nc.vector.memset(sel[:], 0.0).then_inc(dve_const, 1)
            for i in range(2):
                nc.vector.memset(nmax_hl[i][:], 0.0)
            for i in range(7):
                nc.vector.memset(xrow[i][:, IDCOL:ROW], 0.0)
            nc.vector.memset(counted[:], 0.0)
            nc.vector.memset(fill[:], 0.0).then_inc(dve_const, 1)
            dve.wait_ge(dve_const, 2)
            nc.vector.memset(fill[:, IDCOL:IDCOL + 1].bitcast(I32), S).then_inc(dve_const, 1)
            dve.wait_ge(const_ld, 32)
            nc.vector.tensor_copy(klen_f[:], klen_i[:]).then_inc(dve_const, 1)
            dve.wait_ge(pool_const, 5)
            nc.vector.tensor_copy(tok[:], tok_i[:])
            nc.vector.tensor_copy(e_f[:], e_i[:]).then_inc(dve_const, 1)
            dve.wait_ge(dve_const, 5)
            nc.vector.tensor_scalar(e_row0[:], e_f[:], float(CAP), None, ALU.mult).then_inc(dve_const, 1)
            dve.wait_ge(sharp_ln, 1)
            nc.vector.tensor_scalar(sharp[:], sharp[:], SCALE, None, ALU.mult).then_inc(dve_const, 1)
            dve.wait_ge(zeroed, 4)
            for i in range(4):
                nc.vector.tensor_copy(kst[i][STACK:P], sel[STACK:P]).then_inc(sel_ready, 1)
            dve.wait_ge(dve_const, 7)

            def bcast(ap, shape):
                return ap.unsqueeze(len(shape) - 1).to_broadcast(shape)

            for s in slots(dve):
                def batch(lag):
                    return s.it * (U // 2) + ((s.k - lag) // 2 + 1)

                for j in range(HPG):
                    if j == 0 and s.has(LN + 1):
                        s.wait(dve, lg_done, LN + 1)
                        nc.vector.tensor_copy(lg[s.ring(LN + 1, 4) // 2][:, s.ring(LN + 1, 2), :], ps_b[:, 0:E]
                                              ).then_inc(lg_saved, 1)
                    if j == 1 and s.has(PREP):
                        s.wait(dve, stat1, PREP)
                    if j == 3 and s.has(OUT):
                        s.wait(dve, stat2, OUT)
                    if s.has(0):
                        for c in range(NC4):
                            s.wait(dve, s_done, 0, each=16, minus=15 - (4 * j + c))
                            if j == 0 and c == 0:
                                s.wait(dve, nmax_ready, 2)
                            nc.vector.tensor_reduce(nmax[s.ring(0, 2)][:, c, j:j + 1], ps_s[c % 2][:], AX, ALU.max,
                                                    negate=True).then_inc(max_done, 1)
                    if j == 0 and s.has(OUT):
                        s.wait(dve, lt_done, OUT)
                        s.wait(dve, r_done, OUT + 2)
                        nc.vector.reciprocal(
                            linv[s.ring(OUT, 2)][:],
                            ps_a[:].rearrange("p (c h d) -> p c h d", c=NC4, d=HD)[:, :, :, 0]).then_inc(linv_ready, 1)
                    if j == 0 and s.has(1):
                        s.wait(dve, m_done, 1)
                        if s.has(2):
                            dve.wait_ge(mrow_ld[s.ring(2, 4)], s.rounds(2, 4) * 16)
                        nc.vector.tensor_copy(mrow[:], ps_b[0:HD, :]).then_inc(mrow_ready, 1)
                    if j == 0 and s.has(PREP):
                        i = s.ring(PREP, 2)
                        dve.wait_ge(x_ld[s.ring(PREP, 8)], s.rounds(PREP, 8) * 16)
                        nc.vector.bn_stats(st1[i][:, 0:6], xt[s.ring(PREP, 8)][:]).then_inc(stat1, 1)
                    if j == 1 and s.has(PREP):
                        i, t = s.ring(PREP, 2), xt[s.ring(PREP, 8)]
                        nc.vector.bn_aggr(st1[i][:, 6:8], st1[i][:, 0:6]).then_inc(var1, 1)
                        s.wait(dve, var1, PREP)
                        nc.vector.tensor_scalar(st1[i][:, 8:9], st1[i][:, 7:8], EPS, None, ALU.add).then_inc(veps1, 1)
                        s.wait(dve, rstd1, PREP)
                        b = s.it * (U // 2) + (s.k - PREP) // 2
                        nc.vector.tensor_tensor(st1[i][:, 10:11], st1[i][:, 9:10], sharp[:, bass.ds(b, 1)],
                                                ALU.mult).then_inc(rs1, 1)
                        s.wait(dve, rs1, PREP)
                        s.wait(dve, qlo_ready, PREP + 1)
                        nc.vector.tensor_scalar(qf[:], t[:], st1[i][:, 6:7], st1[i][:, 10:11],
                                                ALU.subtract, ALU.mult).then_inc(q_ready, 1)
                    if j == 2 and s.has(OUT):
                        i = s.ring(OUT, 2)
                        s.wait(dve, r_done, OUT)
                        s.wait(dve, o_saved, OUT)
                        nc.vector.tensor_tensor(o_sb[:], ps_a[:], o_sb[:], ALU.mult).then_inc(scaled, 1)
                        s.wait(dve, scaled, OUT)
                        if s.has(OUT + 2):
                            dve.wait_ge(x1_st[i], s.rounds(OUT + 2, 2) * 16)
                        nc.vector.tensor_tensor(x1[i][:], o_sb[:], xt[s.ring(OUT, 8)][:], ALU.add).then_inc(x1_ready, 1)
                        s.wait(dve, x1_ready, OUT)
                        nc.vector.bn_stats(st2[i][:, 0:6], x1[i][:]).then_inc(stat2, 1)
                    if j == 3 and s.has(OUT):
                        i = s.ring(OUT, 2)
                        nc.vector.bn_aggr(st2[i][:, 6:8], st2[i][:, 0:6]).then_inc(var2, 1)
                        s.wait(dve, var2, OUT)
                        nc.vector.tensor_scalar(st2[i][:, 8:9], st2[i][:, 7:8], EPS, None, ALU.add).then_inc(veps2, 1)
                    if j == 3 and s.has(0):
                        i = s.ring(0, 2)
                        s.wait(dve, max_done, 0, each=16)
                        s.wait(dve, m_done, 2)
                        nc.vector.tensor_copy(nmax_hl[i][:, :, 0:HPG].bitcast(F32R), nmax[i][:]).then_inc(nmax_hi, 1)
                        s.wait(dve, nmax_hi, 0)
                        nc.vector.tensor_tensor(nmax_hl[i][:, :, HPG:MROWS], nmax[i][:], nmax_hl[i][:, :, 0:HPG],
                                                ALU.subtract).then_inc(nmax_ready, 1)
                    if j == 3 and s.has(OUT):
                        i, r = s.ring(OUT, 2), s.ring(OUT, 8)
                        s.wait(dve, rstd2, OUT)
                        if r == 7:
                            dve.wait_ge(fill_st, 16 * E)
                        nc.vector.tensor_scalar(xrow[r][:, 0:D], x1[i][:], st2[i][:, 6:7], st2[i][:, 9:10],
                                                ALU.subtract, ALU.mult).then_inc(x2_ready, 1)
                    if j == 1 and s.k % 2 and s.has(7):
                        n = batch(7)
                        i = s.ring(7, 4) // 2
                        s.wait(dve, lg_saved, LN + 1)
                        nc.vector.reduce_max(lmax[:], lg[i][:], AX).then_inc(rt["lmax"], 1)
                        dve.wait_ge(rt["lmax"], n)
                        nc.vector.tensor_tensor(lsub[:], lg[i][:], bcast(lmax[:], [P, 2, E]), ALU.subtract
                                                ).then_inc(rt["lsub"], 1)
                    if j == 0 and s.k % 2 == 0 and s.has(8):
                        n = batch(8)
                        dve.wait_ge(rt["lexp"], n)
                        nc.vector.reduce_sum(zsum[:], lexp[:], AX).then_inc(rt["zsum"], 1)
                        dve.wait_ge(rt["zsum"], n)
                        nc.vector.reciprocal(zinv[:], zsum[:]).then_inc(rt["zinv"], 1)
                        dve.wait_ge(rt["zinv"], n)
                        nc.vector.tensor_tensor(pr[:], lexp[:], bcast(zinv[:], [P, 2, E]), ALU.mult
                                                ).then_inc(rt["pr"], 1)
                        dve.wait_ge(rt["pr"], n)
                        nc.vector.tensor_copy(before[:, 0, :], counted[:]).then_inc(rt["first"], 1)
                        for h in range(2):
                            nc.vector.max(top[:, h, :], pr[:, h, :]).then_inc(rt["top"], 1)
                        dve.wait_ge(rt["top"], n * 2)
                        for h in range(2):
                            nc.vector.tensor_scalar(xrow[s.ring(8 - h, 8)][:, IDCOL:IDCOL + 1].bitcast(I32),
                                                    tok[:, bass.ds(s.group(8 - h), 1)], 1.0, None, ALU.mult)
                        for h in range(2):
                            nc.vector.max_index(topi[:, h, :], top[:, h, :], pr[:, h, :]).then_inc(rt["topi"], 1)
                        dve.wait_ge(rt["topi"], n * 2)
                        nc.vector.tensor_copy(topf[:], topi[:, :, 0:TOPK]).then_inc(rt["topf"], 1)
                        dve.wait_ge(rt["topf"], n)
                        for h in range(2):
                            nc.vector.tensor_tensor(hot[:, h], e_f[:].unsqueeze(1).to_broadcast([P, TOPK, E]),
                                                    bcast(topf[:, h, :], [P, TOPK, E]), ALU.is_equal
                                                    ).then_inc(rt["hot"], 1)
                        dve.wait_ge(rt["hot"], n * 2)
                        nc.vector.tensor_tensor(picked[:], hot[:, :, 0, :], hot[:, :, 1, :], ALU.add
                                                ).then_inc(rt["picked"], 1)
                        dve.wait_ge(rt["picked"], n)
                        dve.wait_ge(rt["first"], n)
                        nc.vector.tensor_tensor(before[:, 1, :], before[:, 0, :], picked[:, 0, :], ALU.add
                                                ).then_inc(rt["before"], 1)
                        dve.wait_ge(rt["before"], n)
                        nc.vector.tensor_tensor(counted[:], before[:, 1, :], picked[:, 1, :], ALU.add
                                                ).then_inc(rt["counted"], 1)
                        dve.wait_ge(rt["counted"], n)
                    if j == 3 and s.k % 2 == 0 and s.has(8):
                        n = batch(8)
                        dve.wait_ge(rt["pos"], n)
                        pos = ps_b[:, 0:2 * E].rearrange("p (h e) -> p h e", h=2)
                        nc.vector.tensor_scalar(over[:], pos, float(CAP), float(1 << 20), ALU.is_ge, ALU.mult
                                                ).then_inc(rt["over"], 1)
                        nc.vector.tensor_tensor(place[:], pos, e_row0[:].unsqueeze(1).to_broadcast([P, 2, E]), ALU.add
                                                ).then_inc(rt["place0"], 1)
                        dve.wait_ge(rt["over"], n)
                        dve.wait_ge(rt["place0"], n)
                        nc.vector.tensor_tensor(place[:], place[:], over[:], ALU.add).then_inc(rt["place"], 1)
                        dve.wait_ge(rt["place"], n)
                        for h in range(2):
                            nc.vector.tensor_tensor(chosen[:, h], hot[:, h],
                                                    place[:, h, :].unsqueeze(1).to_broadcast([P, TOPK, E]), ALU.mult
                                                    ).then_inc(rt["chosen"], 1)
                        dve.wait_ge(rt["chosen"], n * 2)
                        nc.vector.reduce_sum(rowf[:], chosen[:], AX).then_inc(rt["rowf"], 1)
                        dve.wait_ge(rt["rowf"], n)
                        nc.vector.tensor_copy(rowd[s.ring(8, 4) // 2][:], rowf[:].rearrange("p h k -> p (h k)")
                                              ).then_inc(rt["rowd"], 1)
                        for h in range(2):
                            last = nc.vector.tensor_tensor(xrow[s.ring(8 - h, 8)][:, GATE0:GATE0 + E], pr[:, h, :],
                                                           picked[:, h, :], ALU.mult)
                        last.then_inc(rt["gate"], 1)
            dve.wait_ge(total_done, 1)
            nc.vector.tensor_copy(totals[:], ps_a[:, 0:E]).then_inc(total_ready, 1)
            dve.wait_ge(total_ready, 1)

        @block.tensor
        def _(pe):
            pe.wait_ge(pool_const, 5)
            pe.wait_ge(sel_ready, 4)
            pe.wait_ge(const_ld, 32)
            for s in slots(pe):
                for j in range(HPG):
                    for c in range(NC4):
                        cols = slice(P * c, P * c + P)
                        if s.has(0):
                            i = s.ring(0, 4)
                            if j == 0 and c == 0:
                                pe.wait_ge(stack_ld[i], s.rounds(0, 4) * (16 * 24))
                            s.wait(pe, max_done, 0, each=16, minus=17 - (4 * j + c))
                            nc.tensor.matmul(ps_s[c % 2][:], qst[i][0:STACK, j, cols], kst[i][0:STACK, j, :],
                                             start=True, stop=True).then_inc(s_done, 1)
                        if s.has(ST):
                            i = s.ring(ST, 4)
                            if j == 0 and c == 0:
                                pe.wait_ge(mrow_ld[i], s.rounds(ST, 4) * 16)
                            s.wait(pe, exp_done, ST, each=16, minus=17 - (4 * j + c))
                            nc.tensor.matmul(ps_t[c % 2][:], kst[i][0:STACK + MROWS, j, cols],
                                             qst[i][0:STACK + MROWS, j, :], start=True, stop=True).then_inc(st_done, 1)
                    if s.has(PV):
                        i = s.ring(PV, 2)
                        if j == 0:
                            s.wait(pe, exp_done, PV, each=16)
                            s.wait(pe, vt_ready, PV)
                            s.wait(pe, o_saved, PV + 1)
                        for h in range(HPG):
                            hd = slice(HD * h, HD * h + HD)
                            nc.tensor.matmul(ps_o[hd, :], vt[s.ring(PV, 4)][:, j, hd], probs[i][:, h, j, :],
                                             start=(j == 0), stop=(j == NC4 - 1))
                        for h in range(HPG):
                            hd = slice(HD * h, HD * h + HD)
                            last = nc.tensor.matmul(ps_l[hd, :], ones[:, 0:HD], probs[i][:, h, j, :],
                                                    start=(j == 0), stop=(j == NC4 - 1))
                        if j == NC4 - 1:
                            last.then_inc(pv_done, 1)
                    if j == 0 and s.has(OUT):
                        s.wait(pe, l_saved, OUT)
                        s.wait(pe, vt_ready, 1)
                        s.wait(pe, scaled, OUT + 1)
                        for c in range(NC4):
                            last = nc.tensor.transpose(ps_a[:, P * c:P * c + P], l_sb[:, P * c:P * c + P],
                                                       ident[:])
                        last.then_inc(lt_done, 1)
                    if j == 0 and s.has(1):
                        s.wait(pe, nmax_ready, 1)
                        s.wait(pe, mrow_ready, 2)
                        s.wait(pe, lg_saved, LN + 1)
                        for c in range(NC4):
                            last = nc.tensor.matmul(ps_b[0:HD, P * c:P * c + P], nmax_hl[s.ring(1, 2)][:, c, :], ident[:],
                                                    start=True, stop=True)
                        last.then_inc(m_done, 1)
                    if j == 1 and s.has(0):
                        if s.has(OUT):
                            s.wait(pe, linv_ready, OUT)
                        s.wait(pe, vt_ready, 1)
                        s.wait(pe, scaled, OUT + 1)
                        pe.wait_ge(c_ld[s.ring(0, 4)], s.rounds(0, 4) * 16)
                        for c in range(NC4):
                            last = nc.tensor.transpose(ps_a[:, P * c:P * c + P], ct[s.ring(0, 4)][:, P * c:P * c + P],
                                                       ident[:])
                        last.then_inc(vt_done, 1)
                    if j == 1 and s.has(LN):
                        s.wait(pe, mrow_ready, 1)
                        s.wait(pe, lg_saved, LN + 1)
                        s.wait(pe, x2_ready, LN)
                        for c in range(NC4):
                            last = nc.tensor.transpose(ps_b[:, P * c:P * c + P], xrow[s.ring(LN, 8)][:, P * c:P * c + P],
                                                       ident[:])
                        last.then_inc(x2t_done, 1)
                    if j == 2 and s.has(OUT):
                        s.wait(pe, vt_ready, 0)
                        s.wait(pe, linv_ready, OUT)
                        for c in range(NC4):
                            for h in range(HPG):
                                last = nc.tensor.matmul(
                                    ps_a[HD * h:HD * h + HD, P * c:P * c + P],
                                    linv[s.ring(OUT, 2)][:, c, h:h + 1].to_broadcast([P, HD]),
                                    ident[:], start=True, stop=True)
                        last.then_inc(r_done, 1)
                    if j == 2 and s.k % 2 == 0 and s.has(8):
                        n = s.it * (U // 2) + ((s.k - 8) // 2 + 1)
                        s.wait(pe, x2t_ready, LN)
                        s.wait(pe, lg_saved, LN + 1)
                        s.wait(pe, mrow_ready, 1)
                        pe.wait_ge(rt["before"], n)
                        pos = ps_b[:, 0:2 * E]
                        nc.tensor.matmul(pos, earlier[:], picked[:].rearrange("p h e -> p (h e)"), start=True, stop=False)
                        nc.tensor.matmul(pos, ones[:], before[:].rearrange("p h e -> p (h e)"), start=False, stop=True
                                         ).then_inc(rt["pos"], 1)
                    if j == 3 and s.has(LN):
                        s.wait(pe, x2t_ready, LN)
                        if s.k % 2 == 0 and s.has(8):
                            n = s.it * (U // 2) + ((s.k - 8) // 2 + 1)
                            pe.wait_ge(rt["place0"], n)
                        for c in range(NC4):
                            last = nc.tensor.matmul(ps_b[:, 0:E], x2t[:, P * c:P * c + P], wg_sb[:, c, :],
                                                    start=(c == 0), stop=(c == NC4 - 1))
                        last.then_inc(lg_done, 1)
            pe.wait_ge(rt["counted"], B)
            pe.wait_ge(scaled, G)
            nc.tensor.matmul(ps_a[:, 0:E], ones[:], counted[:], start=True, stop=True).then_inc(total_done, 1)


def experts(nc, w1, w2, out_rows, disp, totals):
    N = E * TILES
    with ExitStack() as stack:
        def sb(name, shape, dt=F32):
            return stack.enter_context(nc.sbuf_tensor(name, shape, dt))

        def sem(name):
            return stack.enter_context(nc.semaphore(name))

        ident = sb("ident2", [P, P])
        w1hi = sb("w1hi", [P, NC4, FF], F32R)
        w1lo = sb("w1lo", [P, NC4, FF], F32R)
        w2hi = sb("w2hi", [P, NF, D], F32R)
        w2lo = sb("w2lo", [P, NF, D], F32R)
        raw = [sb(f"raw{i}", [P, 2 * D]) for i in range(NRAW)]
        xin = sb("xin", [P, 2, ROW])
        xhi = sb("xhi", [P, NC4, T], F32R)
        xlo = sb("xlo", [P, NC4, T], F32R)
        hhi = sb("hhi", [P, NF, T], F32R)
        hlo = sb("hlo", [P, NF, T], F32R)
        gates = sb("gates", [P, 2, E])
        ids = sb("ids", [P, 2], I32)
        zeros = sb("zeros2", [P, 2], I32)
        turn = [sb(f"turn{h}", [P, 1], I32) for h in range(2)]
        y = [sb(f"y{h}", [P, D]) for h in range(2)]

        ps_x = [stack.enter_context(nc.psum_tensor(f"ps_x{i}", [P, 2, T], F32)) for i in range(2)]
        ps_h = [stack.enter_context(nc.psum_tensor(f"ps_h{i}", [P, 2, T], F32)) for i in range(4)]
        ps_y = [stack.enter_context(nc.psum_tensor(f"ps_y{i}", [P, D], F32)) for i in range(2)]

        zeroed = sem("zeroed2")
        ident_ready = sem("ident_ready")
        raw_ld = [sem(f"raw_ld{i}") for i in range(NRAW)]
        xin_ld = sem("xin_ld")
        w_hi = sem("w_hi")
        w_ready = sem("w_ready")
        xt_done = sem("xt_done")
        xhi_ready = sem("xhi_ready")
        xlo_ready = sem("xlo_ready")
        gates_kept = sem("gates_kept")
        ids_kept = sem("ids_kept")
        turn_taken = sem("turn_taken")
        h_done = sem("h_done")
        hhi_ready = sem("hhi_ready")
        h_ready = sem("h_ready")
        y_done = sem("y_done")
        y_ready = sem("y_ready")
        y_added = sem("y_added")

        disp_t = disp.rearrange("(n h p) w -> n p h w", h=2, p=P)
        w1_p = w1.rearrange("e (c p) f -> e c p f", p=P)
        w2_p = w2.rearrange("e (f p) d -> e p f d", p=P)
        HALF = FF // 2

        def piece(t1, t2, i):
            if i < 8:
                return t1[:, i % NC4, HALF * (i // NC4):HALF * (i // NC4) + HALF]
            f = 2 * (i - 8)
            return t2[:, f:f + 2, :].rearrange("p f d -> p (f d)")

        def rows_of(eng, e):
            return eng.value_load(totals[0:1, bass.ds(e, 1)], min_val=0, max_val=S)

        block = stack.enter_context(nc.Block())

        @block.sync
        def _(sp):
            def weights(e, pieces, first):
                for i in pieces:
                    if not (first and i < NRAW):
                        sp.wait_ge(w_ready, e * PIECES + (i - NRAW + 1))
                    if i < 8:
                        src = w1_p[bass.ds(e, 1), i % NC4, :, HALF * (i // NC4):HALF * (i // NC4) + HALF].rearrange(
                            "e p f -> (e p) f")
                        dst = raw[i % NRAW][:]
                    else:
                        f = 2 * (i - 8)
                        src = w2_p[bass.ds(e, 1), :, f:f + 2, :].rearrange("e p f d -> (e p) f d")
                        dst = raw[i % NRAW][:].rearrange("p (f d) -> p f d", f=2)
                    sp.dma_start(dst, src).then_inc(raw_ld[i % NRAW], 16)

            def tile_in(n, first=False):
                if not first:
                    sp.wait_ge(xt_done, n * 2)
                    sp.wait_ge(gates_kept, n)
                    sp.wait_ge(ids_kept, n)
                sp.dma_start(xin[:], disp_t[bass.ds(n, 1)].rearrange("n p h w -> (n p) h w")).then_inc(xin_ld, 16)

            tile_in(0, first=True)
            weights(0, range(PIECES), True)
            with sp.Fori(1, TILES) as t:
                tile_in(t)
            with sp.Fori(1, E) as e:
                tile_in(e * TILES)
                weights(e, range(PIECES), False)
                with sp.Fori(1, TILES) as t:
                    tile_in(e * TILES + t)

        @block.gpsimd
        def _(pool):
            nc.gpsimd.memset(zeros[:], 0).then_inc(zeroed, 1)
            nc.gpsimd.memset(ident[:], 0.0).then_inc(zeroed, 1)
            pool.wait_ge(zeroed, 2)
            nc.gpsimd.affine_select(out=ident[:], in_=ident[:], compare_op=ALU.not_equal, fill=1.0, base=0,
                                    pattern=[[-1, P]], channel_multiplier=1).then_inc(ident_ready, 1)

            def tile(n, first=False):
                if not first:
                    pool.wait_ge(turn_taken, n * 2)
                pool.wait_ge(xin_ld, n * 16 + 16)
                nc.gpsimd.tensor_tensor(ids[:], xin[:, :, IDCOL].bitcast(I32), zeros[:], ALU.add).then_inc(ids_kept, 1)
                pool.wait_ge(ids_kept, n + 1)
                for h in range(2):
                    pool.wait_ge(y_ready, n * 2 + (h + 1))
                    nc.gpsimd.tensor_tensor(turn[h][:], ids[:, h:h + 1], zeros[:, 0:1], ALU.add).then_inc(turn_taken, 1)
                    nc.gpsimd.indirect_dma_start(
                        out=out_rows[:, :], in_=y[h][:], in_offset=None,
                        out_offset=bass.IndirectOffsetOnAxis(ap=ids[:, h:h + 1].bitcast(U32), axis=0),
                        bounds_check=S - 1, oob_is_err=False, compute_op=ALU.add).then_inc(y_added, 16)
                    pool.wait_ge(y_added, n * 32 + 16 * (h + 1))

            tile(0, first=True)
            with pool.Fori(1, N) as n:
                tile(n)

        @block.scalar
        def _(act):
            def cut(e, i):
                act.wait_ge(raw_ld[i % NRAW], e * (16 * PIECES // NRAW) + 16 * (i // NRAW + 1))
                nc.scalar.activation(piece(w1hi, w2hi, i), raw[i % NRAW][:], ACT.Copy).then_inc(w_hi, 1)

            def x_in(n):
                for i in range(2):
                    act.wait_ge(xt_done, n * 2 + (i + 1))
                    nc.scalar.activation(xhi[:, 2 * i:2 * i + 2, :], ps_x[i][:], ACT.Copy).then_inc(xhi_ready, 1)

            def tile(n, e=None, free=True):
                for f in range(NF // 2):
                    act.wait_ge(h_done, n * 8 + (f + 1))
                    nc.scalar.activation(hhi[:, 2 * f:2 * f + 2, :], ps_h[f % 4][:], ACT.Relu).then_inc(hhi_ready, 1)
                    if e is not None:
                        if free and f == 0:
                            act.wait_ge(y_done, n * 2)
                        cut(e, 8 + f)

            def later_tiles(e):
                rows = rows_of(act, e)
                with act.Fori(1, TILES) as t:
                    n = e * TILES + t
                    x_in(n)
                    with act.If(rows > t * T):
                        tile(n)
                    with act.Else():
                        act.wait_ge(hhi_ready, n * 8)
                        act.sem_inc(hhi_ready, 8)

            x_in(0)
            for i in range(8):
                cut(0, i)
            tile(0, 0, free=False)
            later_tiles(0)
            with act.Fori(1, E) as e:
                x_in(e * TILES)
                for i in range(8):
                    cut(e, i)
                tile(e * TILES, e)
                later_tiles(e)

        @block.vector
        def _(dve):
            def cut(e, i):
                dve.wait_ge(w_hi, e * PIECES + (i + 1))
                nc.vector.tensor_tensor(piece(w1lo, w2lo, i), raw[i % NRAW][:], piece(w1hi, w2hi, i).bitcast(F32),
                                        ALU.subtract).then_inc(w_ready, 1)

            def x_in(n):
                for i in range(2):
                    dve.wait_ge(xhi_ready, n * 2 + (i + 1))
                    nc.vector.tensor_tensor(xlo[:, 2 * i:2 * i + 2, :], ps_x[i][:],
                                            xhi[:, 2 * i:2 * i + 2, :].bitcast(F32), ALU.subtract).then_inc(xlo_ready, 1)

            def y_half(n, e, h):
                dve.wait_ge(y_done, n * 2 + (h + 1))
                dve.wait_ge(gates_kept, n + 1)
                nc.vector.tensor_scalar(y[h][:], ps_y[h][:], gates[:, h, bass.ds(e, 1)], None, ALU.mult
                                        ).then_inc(y_ready, 1)

            def y_out_first(n, e, free=True):
                for h in range(2):
                    if free:
                        dve.wait_ge(y_added, n * 32 + (16 * h - 16))
                    y_half(n, e, h)

            def y_out(n, e, t, rows):
                for h in range(2):
                    with dve.If(rows > t * T + P * h):
                        dve.wait_ge(y_added, n * 32 + (16 * h - 16))
                        y_half(n, e, h)
                    with dve.Else():
                        dve.wait_ge(y_ready, n * 2 + h)
                        dve.sem_inc(y_ready, 1)

            def keep_gates(n, first=False):
                if not first:
                    dve.wait_ge(y_ready, n * 2)
                dve.wait_ge(xin_ld, n * 16 + 16)
                nc.vector.tensor_copy(gates[:], xin[:, :, GATE0:GATE0 + E]).then_inc(gates_kept, 1)

            def h_low(n, e=None):
                for f in range(NF // 2):
                    dve.wait_ge(hhi_ready, n * 8 + (f + 1))
                    nc.vector.scalar_tensor_tensor(hlo[:, 2 * f:2 * f + 2, :], ps_h[f % 4][:], 0.0,
                                                   hhi[:, 2 * f:2 * f + 2, :].bitcast(F32), ALU.max, ALU.subtract
                                                   ).then_inc(h_ready, 1)
                    if e is not None:
                        cut(e, 8 + f)

            def later_h_low(n, t, rows):
                with dve.If(rows > t * T):
                    h_low(n)
                with dve.Else():
                    dve.wait_ge(h_ready, n * 8)
                    dve.sem_inc(h_ready, 8)

            def later_tiles(e, first=False):
                rows = rows_of(dve, e)
                x_in(e * TILES + 1)
                y_out_first(e * TILES, e, free=not first)
                keep_gates(e * TILES + 1)
                later_h_low(e * TILES + 1, 1, rows)
                with dve.Fori(2, TILES) as t:
                    n = e * TILES + t
                    x_in(n)
                    y_out(n - 1, e, t - 1, rows)
                    keep_gates(n)
                    later_h_low(n, t, rows)

            x_in(0)
            for i in range(8):
                cut(0, i)
            keep_gates(0, first=True)
            h_low(0, 0)
            later_tiles(0, first=True)
            with dve.Fori(1, E) as e:
                x_in(e * TILES)
                for i in range(8):
                    cut(e, i)
                y_out(e * TILES - 1, e - 1, TILES - 1, rows_of(dve, e - 1))
                keep_gates(e * TILES)
                h_low(e * TILES, e)
                later_tiles(e)
            y_out(N - 1, E - 1, TILES - 1, rows_of(dve, E - 1))

        @block.tensor
        def _(pe):
            pe.wait_ge(ident_ready, 1)

            def x_in(n, first=False):
                pe.wait_ge(xin_ld, n * 16 + 16)
                if not first:
                    pe.wait_ge(xlo_ready, n * 2)
                for i in range(2):
                    for c in range(2):
                        for h in range(2):
                            k = 2 * i + c
                            last = nc.tensor.transpose(ps_x[i][:, c, P * h:P * h + P], xin[:, h, P * k:P * k + P], ident[:])
                    last.then_inc(xt_done, 1)

            def up(n, e=None, first=False):
                pe.wait_ge(xlo_ready, n * 2 + 2)
                for f in range(NF):
                    if e is not None and f % 8 == 0:
                        pe.wait_ge(w_ready, e * PIECES + (NC4 * (f // 8) + NC4))
                    if f % 2 == 0 and not (first and f < 8):
                        pe.wait_ge(h_ready, n * 8 + (f // 2 - 3))
                    fs = slice(P * f, P * f + P)
                    to = ps_h[f // 2 % 4][:, f % 2, :]
                    for c in range(NC4):
                        nc.tensor.matmul(to, w1hi[:, c, fs], xhi[:, c, :], start=(c == 0), stop=False)
                        nc.tensor.matmul(to, w1hi[:, c, fs], xlo[:, c, :], start=False, stop=False)
                        last = nc.tensor.matmul(to, w1lo[:, c, fs], xhi[:, c, :], start=False, stop=(c == NC4 - 1))
                    if f % 2:
                        last.then_inc(h_done, 1)

            def down(n, h, e=None, first=False):
                if not first:
                    pe.wait_ge(y_ready, n * 2 + (h - 1))
                hs = slice(P * h, P * h + P)
                for f in range(NF):
                    if h == 0 and f % 2 == 0:
                        pe.wait_ge(h_ready, n * 8 + (f // 2 + 1))
                        if e is not None:
                            pe.wait_ge(w_ready, e * PIECES + (8 + f // 2 + 1))
                    nc.tensor.matmul(ps_y[h][:], hhi[:, f, hs], w2hi[:, f, :], start=(f == 0), stop=False)
                    nc.tensor.matmul(ps_y[h][:], hhi[:, f, hs], w2lo[:, f, :], start=False, stop=False)
                    last = nc.tensor.matmul(ps_y[h][:], hlo[:, f, hs], w2hi[:, f, :], start=False, stop=(f == NF - 1))
                last.then_inc(y_done, 1)

            def later_tile(e, t, rows, next_in=True):
                n = e * TILES + t
                with pe.If(rows > t * T):
                    up(n)
                with pe.Else():
                    pe.wait_ge(h_done, n * 8)
                    pe.sem_inc(h_done, 8)
                if next_in:
                    x_in(n + 1)
                for h in range(2):
                    with pe.If(rows > t * T + P * h):
                        down(n, h)
                    with pe.Else():
                        pe.wait_ge(y_done, n * 2 + h)
                        pe.sem_inc(y_done, 1)

            x_in(0, first=True)
            up(0, 0, first=True)
            x_in(1)
            down(0, 0, 0, first=True)
            down(0, 1, 0, first=True)
            rows0 = rows_of(pe, 0)
            with pe.Fori(1, TILES) as t:
                later_tile(0, t, rows0)
            with pe.Fori(1, E - 1) as e:
                rows = rows_of(pe, e)
                up(e * TILES, e)
                x_in(e * TILES + 1)
                down(e * TILES, 0, e)
                down(e * TILES, 1, e)
                with pe.Fori(1, TILES) as t:
                    later_tile(e, t, rows)
            up(N - TILES, E - 1)
            x_in(N - TILES + 1)
            down(N - TILES, 0, E - 1)
            down(N - TILES, 1, E - 1)
            rows7 = rows_of(pe, E - 1)
            with pe.Fori(1, TILES - 1) as t:
                later_tile(E - 1, t, rows7)
            later_tile(E - 1, TILES - 1, rows7, next_in=False)


_INS = ["x", "ctx_2048", "itok_B_779_1933", "L0_ffn_Wg", "L0_ffn_w1", "L0_ffn_w2"]


def kernel(**inputs):
    import concourse.bacc as bacc
    from concourse.bass_utils import run_bass_kernel_spmd

    nc = bacc.Bacc("TRN2", target_bir_lowering=False, num_devices=1, dynamic_dma_scratch_size=8192)
    arrays, args = {}, []
    for name in _INS:
        a = np.ascontiguousarray(inputs[name])
        arrays[f"in_{name}"] = a
        args.append(nc.dram_tensor(f"in_{name}", a.shape, mybir.dt.from_np(a.dtype), kind="ExternalInput").ap())
    out = nc.dram_tensor("out_x", (B, CH, D), F32, kind="ExternalOutput").ap()
    disp = nc.dram_tensor("dispatched", (E * CAP, ROW), F32, kind="Internal").ap()
    layer(nc, *args, out, disp)
    r = run_bass_kernel_spmd(nc, [arrays], core_ids=[0])
    return r.results[0]["out_x"]
```

```python
from contextlib import ExitStack

import concourse.bass as bass
import numpy as np
from concourse import mybir

F32 = mybir.dt.float32
F32R = mybir.dt.float32r
I32 = mybir.dt.int32
U32 = mybir.dt.uint32
ALU = mybir.AluOpType
ACT = mybir.ActivationFunctionType
AX = mybir.AxisListType.X

P = 128
B, CH, D = 16, 256, 512
HEADS = 8
HD = CH // HEADS
HPG = P // HD
G = B * CH // P
S = B * CH
NC4 = D // P
E, TOPK, FF = 8, 2, 2048
CAP = -(-5 * S * TOPK // (4 * E))
T = 256
TILES = CAP // T
NF = FF // P
ROW = 528
GATE0, IDCOL = D, D + E
EPS = 1e-5
SCALE = 1.0 / (64 ** 0.5 * float(np.log(20)))
U = 8
STACK = 3 * HD
COPIES = 6
MROWS = 2 * HPG
PIECES = 16
NRAW = 4

PREP, LOADX = -2, -3
ST, PV, OUT, LN = 2, 3, 4, 5
RES = 2


class Slot:

    def __init__(self, it, k):
        self.it, self.k = it, k

    def has(self, lag):
        if not isinstance(self.it, int):
            return True
        return 0 <= U * self.it + self.k - lag < G

    def group(self, lag):
        return self.it * U + (self.k - lag)

    def rounds(self, lag, ring):
        g = self.k - lag
        return self.it * (U // ring) + (g // ring + 1)

    def ring(self, lag, ring):
        return (self.k - lag) % ring

    def wait(self, eng, sem, lag, each=1, minus=0, ahead=False):
        if not isinstance(self.it, int):
            eng.wait_ge(sem, self.it * (U * each) + ((self.k - lag + 1) * each - minus))
            return
        g = min(U * self.it + self.k - lag, G - 1)
        if (g + 1) * each - minus > 0:
            eng.wait_ge(sem, (g + 1) * each - minus)


def slots(eng):
    for k in range(LOADX, U):
        yield Slot(k // U, k % U)
    with eng.Fori(1, G // U - 1) as it:
        for k in range(U):
            yield Slot(it, k)
    for k in range(G - U, G + U + 2):
        yield Slot(k // U, k % U)


def layer(nc, x, ctx, klen, wg, w1, w2, out, disp):
    x_rows = x.rearrange("b c l -> (b c) l")
    ctx_rows = ctx.rearrange("b c l -> (b c) l")
    out_rows = out.rearrange("b c l -> (b c) l")
    with nc.sbuf_tensor("totals", [P, E], I32) as totals:
        attention_and_dispatch(nc, x_rows, ctx_rows, klen, wg, out_rows, disp, totals)
        experts(nc, w1, w2, out_rows, disp, totals)


def attention_and_dispatch(nc, x_rows, ctx_rows, klen, wg, out_rows, disp, totals):
    with ExitStack() as stack:
        def sb(name, shape, dt=F32):
            return stack.enter_context(nc.sbuf_tensor(name, shape, dt))

        def sem(name):
            return stack.enter_context(nc.semaphore(name))

        def sems(name, n):
            return [sem(f"{name}{i}") for i in range(n)]

        ident = sb("ident", [P, P])
        ones = sb("ones", [P, P])
        earlier = sb("earlier", [P, P])
        wg_sb = sb("wg_sb", [P, NC4, E])
        klen_i = sb("klen_i", [P, B], I32)
        klen_f = sb("klen_f", [P, B])
        sharp = sb("sharp", [P, B])
        nhalf = sb("nhalf", [P, 1])
        tok_i = sb("tok_i", [P, G], I32)
        tok = sb("tok", [P, G])
        e_i = sb("e_i", [P, E], I32)
        e_f = sb("e_f", [P, E])
        e_row0 = sb("e_row0", [P, E])
        counted = sb("counted", [P, E])

        xt = [sb(f"xt{i}", [P, D]) for i in range(4)]
        xres = [sb(f"xres{i}", [P, D]) for i in range(4)]
        ct = [sb(f"ct{i}", [P, D]) for i in range(4)]
        qst = [sb(f"qst{i}", [P, HPG, D], F32R) for i in range(4)]
        kst = [sb(f"kst{i}", [P, HPG, D], F32R) for i in range(4)]
        probs = [sb(f"probs{i}", [P, HPG, NC4, D]) for i in range(2)]
        sel = probs[0][:, 0]
        vt = [sb(f"vt{i}", [P, NC4, P]) for i in range(4)]
        qf = sb("qf", [P, D])
        qhi = [sb(f"qhi{i}", [P, D], F32R) for i in range(2)]
        qlo = [sb(f"qlo{i}", [P, D], F32R) for i in range(2)]
        khi = [sb(f"khi{i}", [P, D], F32R) for i in range(2)]
        klo = [sb(f"klo{i}", [P, D], F32R) for i in range(2)]
        st1 = [sb(f"st1_{i}", [P, 12]) for i in range(2)]
        nmax = [sb(f"nmax{i}", [P, NC4, HPG]) for i in range(2)]
        nmax_hl = [sb(f"nmax_hl{i}", [P, NC4, HD]) for i in range(2)]
        mrow = sb("mrow", [HD, D], F32R)
        o_sb = sb("o_sb", [P, D])
        l_sb = sb("l_sb", [P, D])
        linv = [sb(f"linv{i}", [P, NC4, HPG]) for i in range(2)]
        x1 = [sb(f"x1_{i}", [P, D]) for i in range(2)]
        st2 = [sb(f"st2_{i}", [P, 12]) for i in range(2)]
        xrow = [sb(f"xrow{i}", [P, ROW]) for i in range(8)]
        x2t = sb("x2t", [P, D])
        fill = xrow[7]
        lg = [sb(f"lg{i}", [P, 2, E]) for i in range(2)]
        lmax = sb("lmax", [P, 2])
        lsub = sb("lsub", [P, 2, E])
        lexp = sb("lexp", [P, 2, E])
        zsum = sb("zsum", [P, 2])
        zinv = sb("zinv", [P, 2])
        pr = sb("pr", [P, 2, E])
        top = sb("top", [P, 2, 8])
        topi = sb("topi", [P, 2, 8], U32)
        topf = sb("topf", [P, 2, TOPK])
        hot = sb("hot", [P, 2, TOPK, E])
        picked = sb("picked", [P, 2, E])
        before = sb("before", [P, 2, E])
        over = sb("over", [P, 2, E])
        place = sb("place", [P, 2, E])
        chosen = sb("chosen", [P, 2, TOPK, E])
        rowf = sb("rowf", [P, 2, TOPK])
        rowd = [sb(f"rowd{i}", [P, 2 * TOPK], I32) for i in range(2)]
        zeros = sb("zeros", [P, 2 * TOPK], I32)
        rowi = [sb(f"rowi{i}", [P, 2 * TOPK], I32) for i in range(2)]

        ps_s = [stack.enter_context(nc.psum_tensor(f"ps_s{i}", [P, D], F32)) for i in range(2)]
        ps_t = [stack.enter_context(nc.psum_tensor(f"ps_t{i}", [P, D], F32)) for i in range(2)]
        ps_o = stack.enter_context(nc.psum_tensor("ps_o", [P, D], F32))
        ps_l = stack.enter_context(nc.psum_tensor("ps_l", [P, D], F32))
        ps_a = stack.enter_context(nc.psum_tensor("ps_a", [P, D], F32))
        ps_b = stack.enter_context(nc.psum_tensor("ps_b", [P, D], F32))

        const_ld = sem("const_ld")
        zeroed = sem("zeroed")
        pool_const = sem("pool_const")
        dve_const = sem("dve_const")
        sharp_ln = sem("sharp_ln")
        sel_ready = sem("sel_ready")
        fill_st = sem("fill_st")
        x_ld = sems("x_ld", 4)
        res_ld = sems("res_ld", 4)
        c_ld = sems("c_ld", 4)
        stack_ld = sems("stack_ld", 4)
        mrow_ld = sems("mrow_ld", 4)
        x1_st = sems("x1_st", 2)
        row_st = sems("row_st", 8)
        stat1 = sem("stat1"); var1 = sem("var1"); veps1 = sem("veps1"); rstd1 = sem("rstd1")
        rs1 = sem("rs1"); q_ready = sem("q_ready")
        qhi_ready = sem("qhi_ready"); khi_ready = sem("khi_ready")
        qlo_ready = sem("qlo_ready"); klo_ready = sem("klo_ready")
        s_done = sem("s_done")
        max_done = sem("max_done")
        nmax_hi = sem("nmax_hi"); nmax_ready = sem("nmax_ready")
        m_done = sem("m_done"); mrow_ready = sem("mrow_ready")
        st_done = sem("st_done")
        exp_done = sem("exp_done")
        vt_done = sem("vt_done"); vt_ready = sem("vt_ready")
        pv_done = sem("pv_done"); o_saved = sem("o_saved"); l_saved = sem("l_saved")
        lt_done = sem("lt_done"); linv_ready = sem("linv_ready")
        r_done = sem("r_done"); scaled = sem("scaled"); x1_ready = sem("x1_ready")
        stat2 = sem("stat2"); var2 = sem("var2"); veps2 = sem("veps2"); rstd2 = sem("rstd2")
        x2_ready = sem("x2_ready"); zeros_ready = sem("zeros_ready")
        x2t_done = sem("x2t_done"); x2t_ready = sem("x2t_ready")
        lg_done = sem("lg_done"); lg_saved = sem("lg_saved")
        total_done = sem("total_done"); total_ready = sem("total_ready")
        rt = {n: sem("rt_" + n) for n in (
            "lmax", "lsub", "lexp", "zsum", "zinv", "pr", "top", "topi", "topf", "hot", "picked", "first",
            "before", "counted", "pos", "place0", "over", "place", "chosen", "rowf", "rowd", "rowi", "gate")}

        def by_dim(rows, g):
            return rows[bass.ds(g * P, P), :].rearrange("(h d) l -> d h l", h=HPG)

        block = stack.enter_context(nc.Block())

        @block.sync
        def _(sp):
            sp.dma_start(wg_sb[:], wg.rearrange("(c p) e -> p c e", p=P)).then_inc(const_ld, 16)
            sp.dma_start(klen_i[:], klen.rearrange("(a b) -> a b", a=1).to_broadcast([P, B])).then_inc(const_ld, 16)
            for s in slots(sp):
                if s.has(1):
                    s.wait(sp, mrow_ready, 1)
                    sp.dma_start(qst[s.ring(1, 4)][STACK:STACK + MROWS, :, :].bitcast(F32),
                                 mrow[0:MROWS, :].bitcast(F32).unsqueeze(1).to_broadcast([MROWS, HPG, D])
                                 ).then_inc(mrow_ld[s.ring(1, 4)], 16)
                if s.has(LOADX):
                    s.wait(sp, q_ready, LOADX + 4)
                    sp.dma_start(xt[s.ring(LOADX, 4)][:], by_dim(x_rows, s.group(LOADX))
                                 ).then_inc(x_ld[s.ring(LOADX, 4)], 16)
                    s.wait(sp, vt_done, LOADX + 4)
                    s.wait(sp, klo_ready, LOADX + 4)
                    sp.dma_start(ct[s.ring(LOADX, 4)][:], by_dim(ctx_rows, s.group(LOADX))
                                 ).then_inc(c_ld[s.ring(LOADX, 4)], 16)
                if s.has(RES):
                    s.wait(sp, x1_ready, RES + 4)
                    sp.dma_start(xres[s.ring(RES, 4)][:], x_rows[bass.ds(s.group(RES) * P, P), :]
                                 ).then_inc(res_ld[s.ring(RES, 4)], 16)
                if s.has(OUT + 1):
                    s.wait(sp, x1_ready, OUT + 1)
                    sp.dma_start(out_rows[bass.ds(s.group(OUT + 1) * P, P), :], x1[s.ring(OUT + 1, 2)][:]
                                 ).then_inc(x1_st[s.ring(OUT + 1, 2)], 16)
                if s.has(PREP):
                    s.wait(sp, st_done, PREP + 4, each=16)
                    s.wait(sp, qhi_ready, PREP)
                    s.wait(sp, khi_ready, PREP)
                    s.wait(sp, qlo_ready, PREP)
                    s.wait(sp, klo_ready, PREP)
                    i, j2 = s.ring(PREP, 4), s.ring(PREP, 2)
                    for n, (q, k) in enumerate(((qhi, khi), (qhi, klo), (qlo, khi))):
                        to = slice(HD * n, HD * n + HD)
                        sp.dma_start(qst[i][to].bitcast(F32), q[j2][:].bitcast(F32)).then_inc(stack_ld[i], 16)
                        sp.dma_start(kst[i][to].bitcast(F32), k[j2][:].bitcast(F32)).then_inc(stack_ld[i], 16)
            for n in range(2):
                sp.wait_ge(x1_st[n], 16 * (G // 2))

        @block.gpsimd
        def _(pool):
            nc.gpsimd.memset(ident[:], 0.0).then_inc(zeroed, 1)
            nc.gpsimd.memset(ones[:], 1.0).then_inc(zeroed, 1)
            nc.gpsimd.memset(nhalf[:], -0.5).then_inc(pool_const, 1)
            nc.gpsimd.memset(zeros[:], 0).then_inc(zeros_ready, 1)
            pool.wait_ge(zeros_ready, 1)
            nc.gpsimd.iota(tok_i[:], [[P, G]], base=0, channel_multiplier=1).then_inc(pool_const, 1)
            nc.gpsimd.iota(e_i[:], [[1, E]], base=0, channel_multiplier=0).then_inc(pool_const, 1)
            pool.wait_ge(zeroed, 2)
            nc.gpsimd.affine_select(out=ident[:], in_=ident[:], compare_op=ALU.not_equal, fill=1.0, base=0,
                                    pattern=[[-1, P]], channel_multiplier=1).then_inc(pool_const, 1)
            nc.gpsimd.affine_select(out=earlier[:], in_=ones[:], compare_op=ALU.is_gt, fill=0.0, base=0,
                                    pattern=[[1, P]], channel_multiplier=-1).then_inc(pool_const, 1)
            pool.wait_ge(pool_const, 5)
            pool.wait_ge(dve_const, 1)
            for part in range(2):
                if part:
                    pool.wait_ge(zeroed, 3)
                nc.gpsimd.affine_select(out=sel[STACK:P], in_=sel[STACK:P], compare_op=ALU.not_equal, fill=1.0,
                                        base=-HPG * part, pattern=[[-1, HPG], [0, D]],
                                        channel_multiplier=1).then_inc(zeroed, 1)
            for s in slots(pool):
                if s.has(LN):
                    s.wait(pool, veps2, LN)
                    i = s.ring(LN, 2)
                    nc.gpsimd.tensor_tensor(st2[i][:, 9:10], st2[i][:, 8:9], nhalf[:], ALU.pow).then_inc(rstd2, 1)
                i9 = s.ring(9, 4) // 2
                b9 = s.it * (U // 2) + ((s.k - 9) // 2 + 1)
                if s.k % 2 and s.has(9):
                    pool.wait_ge(rt["rowd"], b9)
                    pool.wait_ge(rt["gate"], b9)
                    nc.gpsimd.tensor_tensor(rowi[i9][:], rowd[i9][:], zeros[:], ALU.add
                                            ).then_inc(rt["rowi"], 1)
                    pool.wait_ge(rt["rowi"], b9)
                if s.has(PREP):
                    i = s.ring(PREP, 2)
                    s.wait(pool, veps1, PREP)
                    nc.gpsimd.tensor_tensor(st1[i][:, 9:10], st1[i][:, 8:9], nhalf[:], ALU.pow).then_inc(rstd1, 1)
                    if s.has(PREP + 2):
                        pool.wait_ge(stack_ld[s.ring(PREP + 2, 4)], s.rounds(PREP + 2, 4) * (16 * COPIES))
                    s.wait(pool, khi_ready, PREP)
                    nc.gpsimd.tensor_tensor(klo[i][:], ct[s.ring(PREP, 4)][:], khi[i][:].bitcast(F32),
                                            ALU.subtract).then_inc(klo_ready, 1)
                    s.wait(pool, qhi_ready, PREP)
                    nc.gpsimd.tensor_tensor(qlo[i][:], qf[:], qhi[i][:].bitcast(F32),
                                            ALU.subtract).then_inc(qlo_ready, 1)
                if s.k % 2 and s.has(9):
                    pool.wait_ge(fill_st, 16 * E)
                    for half in range(2):
                        for k in range(TOPK):
                            r = s.ring(9 - half, 8)
                            nc.gpsimd.indirect_dma_start(
                                out=disp[:, :], in_=xrow[r][:], in_offset=None,
                                out_offset=bass.IndirectOffsetOnAxis(
                                    ap=rowi[i9][:, TOPK * half + k:TOPK * half + k + 1].bitcast(U32), axis=0),
                                bounds_check=E * CAP - 1, oob_is_err=False).then_inc(row_st[r], 16)
                    for half in range(2):
                        pool.wait_ge(row_st[s.ring(9 - half, 8)], s.rounds(9 - half, 8) * (16 * TOPK))

        @block.scalar
        def _(act):
            act.wait_ge(const_ld, 32)
            act.wait_ge(dve_const, 4)
            nc.scalar.activation(sharp[:], klen_f[:], ACT.Ln).then_inc(sharp_ln, 1)
            disp_rows = disp.rearrange("(e n p) w -> e p n w", e=E, p=P)
            for s in slots(act):
                if isinstance(s.it, int) and s.it == 0:
                    act.dma_start(disp_rows[s.k], fill[:].unsqueeze(1).to_broadcast([P, CAP // P, ROW])
                                  ).then_inc(fill_st, 16)
                for j in range(HPG):
                    if j == 0 and s.has(OUT):
                        s.wait(act, pv_done, OUT)
                        s.wait(act, x1_ready, OUT + 1)
                        nc.scalar.activation(o_sb[:], ps_o[:], ACT.Copy).then_inc(o_saved, 1)
                    for c in range(NC4):
                        if s.has(ST):
                            s.wait(act, st_done, ST, each=16, minus=15 - (4 * j + c))
                            if j == 0 and c == 0:
                                s.wait(act, pv_done, ST + 2)
                            nc.scalar.activation(probs[s.ring(ST, 2)][:, j, c, :], ps_t[c % 2][:], ACT.Exp
                                                 ).then_inc(exp_done, 1)
                        if (j, c) == (0, 1) and s.has(OUT):
                            s.wait(act, lt_done, OUT + 1)
                            nc.scalar.activation(l_sb[:], ps_l[:], ACT.Copy).then_inc(l_saved, 1)
                        if (j, c) == (1, 3) and s.has(0):
                            s.wait(act, vt_done, 0)
                            s.wait(act, pv_done, 4)
                            nc.scalar.activation(vt[s.ring(0, 4)][:].rearrange("p c (h d) -> p c d h", h=HPG),
                                                 ps_a[:].rearrange("p (c d h) -> p c d h", c=NC4, h=HPG), ACT.Copy
                                                 ).then_inc(vt_ready, 1)
                        if (j, c) == (2, 1) and s.has(LN):
                            s.wait(act, x2t_done, LN)
                            s.wait(act, lg_done, LN + 1)
                            nc.scalar.activation(x2t[:], ps_b[:], ACT.Copy).then_inc(x2t_ready, 1)
                    if j == 2 and s.has(PREP):
                        if s.has(PREP + 2):
                            act.wait_ge(stack_ld[s.ring(PREP + 2, 4)], s.rounds(PREP + 2, 4) * (16 * COPIES))
                        act.wait_ge(c_ld[s.ring(PREP, 4)], s.rounds(PREP, 4) * 16)
                        nc.scalar.activation(khi[s.ring(PREP, 2)][:], ct[s.ring(PREP, 4)][:], ACT.Copy
                                             ).then_inc(khi_ready, 1)
                        s.wait(act, q_ready, PREP)
                        nc.scalar.activation(qhi[s.ring(PREP, 2)][:], qf[:], ACT.Copy
                                             ).then_inc(qhi_ready, 1)
                    if j == 3 and s.k % 2 and s.has(7):
                        act.wait_ge(rt["lsub"], s.it * (U // 2) + ((s.k - 7) // 2 + 1))
                        nc.scalar.activation(lexp[:], lsub[:], ACT.Exp).then_inc(rt["lexp"], 1)
            act.wait_ge(fill_st, 16 * E)

        @block.vector
        def _(dve):
            nc.vector.memset(sel[:], 0.0).then_inc(dve_const, 1)
            for i in range(2):
                nc.vector.memset(nmax_hl[i][:], 0.0)
            for i in range(7):
                nc.vector.memset(xrow[i][:, IDCOL:ROW], 0.0)
            nc.vector.memset(counted[:], 0.0)
            nc.vector.memset(fill[:], 0.0).then_inc(dve_const, 1)
            dve.wait_ge(dve_const, 2)
            nc.vector.memset(fill[:, IDCOL:IDCOL + 1].bitcast(I32), S).then_inc(dve_const, 1)
            dve.wait_ge(const_ld, 32)
            nc.vector.tensor_copy(klen_f[:], klen_i[:]).then_inc(dve_const, 1)
            dve.wait_ge(pool_const, 5)
            nc.vector.tensor_copy(tok[:], tok_i[:])
            nc.vector.tensor_copy(e_f[:], e_i[:]).then_inc(dve_const, 1)
            dve.wait_ge(dve_const, 5)
            nc.vector.tensor_scalar(e_row0[:], e_f[:], float(CAP), None, ALU.mult).then_inc(dve_const, 1)
            dve.wait_ge(sharp_ln, 1)
            nc.vector.tensor_scalar(sharp[:], sharp[:], SCALE, None, ALU.mult).then_inc(dve_const, 1)
            dve.wait_ge(zeroed, 4)
            for i in range(4):
                nc.vector.tensor_copy(kst[i][STACK:P], sel[STACK:P]).then_inc(sel_ready, 1)
            dve.wait_ge(dve_const, 7)

            def bcast(ap, shape):
                return ap.unsqueeze(len(shape) - 1).to_broadcast(shape)

            for s in slots(dve):
                def batch(lag):
                    return s.it * (U // 2) + ((s.k - lag) // 2 + 1)

                for j in range(HPG):
                    for c in range(NC4):
                        if (j, c) == (0, 0) and s.has(LN):
                            s.wait(dve, stat2, LN)
                        if (j, c) == (0, 3) and s.has(PREP):
                            s.wait(dve, stat1, PREP)
                        if s.has(0):
                            s.wait(dve, s_done, 0, each=16, minus=15 - (4 * j + c))
                            if j == 0 and c == 0:
                                s.wait(dve, nmax_ready, 2)
                            nc.vector.tensor_reduce(nmax[s.ring(0, 2)][:, c, j:j + 1], ps_s[c % 2][:], AX, ALU.max,
                                                    negate=True).then_inc(max_done, 1)
                        if (j, c) == (0, 0) and s.has(LN + 1):
                            s.wait(dve, lg_done, LN + 1)
                            nc.vector.tensor_copy(lg[s.ring(LN + 1, 4) // 2][:, s.ring(LN + 1, 2), :], ps_b[:, 0:E]
                                                  ).then_inc(lg_saved, 1)
                        if (j, c) == (0, 1) and s.has(PREP):
                            i = s.ring(PREP, 2)
                            dve.wait_ge(x_ld[s.ring(PREP, 4)], s.rounds(PREP, 4) * 16)
                            nc.vector.bn_stats(st1[i][:, 0:6], xt[s.ring(PREP, 4)][:]).then_inc(stat1, 1)
                        if (j, c) == (0, 1) and s.has(LN):
                            i = s.ring(LN, 2)
                            nc.vector.bn_aggr(st2[i][:, 6:8], st2[i][:, 0:6]).then_inc(var2, 1)
                            s.wait(dve, var2, LN)
                            nc.vector.tensor_scalar(st2[i][:, 8:9], st2[i][:, 7:8], EPS, None, ALU.add).then_inc(veps2, 1)
                        if (j, c) == (0, 3) and s.has(PREP):
                            i = s.ring(PREP, 2)
                            nc.vector.bn_aggr(st1[i][:, 6:8], st1[i][:, 0:6]).then_inc(var1, 1)
                            s.wait(dve, var1, PREP)
                            nc.vector.tensor_scalar(st1[i][:, 8:9], st1[i][:, 7:8], EPS, None, ALU.add).then_inc(veps1, 1)
                        if (j, c) == (0, 3) and s.has(OUT):
                            s.wait(dve, lt_done, OUT)
                            s.wait(dve, r_done, OUT + 2)
                            nc.vector.reciprocal(
                                linv[s.ring(OUT, 2)][:],
                                ps_a[:].rearrange("p (c h d) -> p c h d", c=NC4, d=HD)[:, :, :, 0]).then_inc(linv_ready, 1)
                        if (j, c) == (0, 3) and s.k % 2 == 0 and s.has(8):
                            n = batch(8)
                            dve.wait_ge(rt["lexp"], n)
                            nc.vector.reduce_sum(zsum[:], lexp[:], AX).then_inc(rt["zsum"], 1)
                            dve.wait_ge(rt["zsum"], n)
                            nc.vector.reciprocal(zinv[:], zsum[:]).then_inc(rt["zinv"], 1)
                            dve.wait_ge(rt["zinv"], n)
                            nc.vector.tensor_tensor(pr[:], lexp[:], bcast(zinv[:], [P, 2, E]), ALU.mult
                                                    ).then_inc(rt["pr"], 1)
                            dve.wait_ge(rt["pr"], n)
                            nc.vector.tensor_copy(before[:, 0, :], counted[:]).then_inc(rt["first"], 1)
                            for h in range(2):
                                nc.vector.max(top[:, h, :], pr[:, h, :]).then_inc(rt["top"], 1)
                            dve.wait_ge(rt["top"], n * 2)
                        if (j, c) == (1, 1) and s.has(1):
                            s.wait(dve, m_done, 1)
                            if s.has(2):
                                dve.wait_ge(mrow_ld[s.ring(2, 4)], s.rounds(2, 4) * 16)
                            nc.vector.tensor_copy(mrow[:], ps_b[0:HD, :]).then_inc(mrow_ready, 1)
                        if (j, c) == (1, 1) and s.has(LN):
                            i, r = s.ring(LN, 2), s.ring(LN, 8)
                            s.wait(dve, rstd2, LN)
                            if r == 7:
                                dve.wait_ge(fill_st, 16 * E)
                            nc.vector.tensor_scalar(xrow[r][:, 0:D], x1[i][:], st2[i][:, 6:7], st2[i][:, 9:10],
                                                    ALU.subtract, ALU.mult).then_inc(x2_ready, 1)
                        if (j, c) == (1, 3) and s.has(PREP):
                            i, t = s.ring(PREP, 2), xt[s.ring(PREP, 4)]
                            s.wait(dve, rstd1, PREP)
                            b = s.it * (U // 2) + (s.k - PREP) // 2
                            nc.vector.tensor_tensor(st1[i][:, 10:11], st1[i][:, 9:10], sharp[:, bass.ds(b, 1)],
                                                    ALU.mult).then_inc(rs1, 1)
                            s.wait(dve, rs1, PREP)
                            s.wait(dve, qlo_ready, PREP + 1)
                            nc.vector.tensor_scalar(qf[:], t[:], st1[i][:, 6:7], st1[i][:, 10:11],
                                                    ALU.subtract, ALU.mult).then_inc(q_ready, 1)
                        if (j, c) == (1, 3) and s.k % 2 and s.has(7):
                            n = batch(7)
                            i = s.ring(7, 4) // 2
                            s.wait(dve, lg_saved, LN + 1)
                            nc.vector.reduce_max(lmax[:], lg[i][:], AX).then_inc(rt["lmax"], 1)
                            dve.wait_ge(rt["lmax"], n)
                            nc.vector.tensor_tensor(lsub[:], lg[i][:], bcast(lmax[:], [P, 2, E]), ALU.subtract
                                                    ).then_inc(rt["lsub"], 1)
                        if (j, c) == (1, 3) and s.k % 2 == 0 and s.has(8):
                            n = batch(8)
                            for h in range(2):
                                nc.vector.tensor_scalar(xrow[s.ring(8 - h, 8)][:, IDCOL:IDCOL + 1].bitcast(I32),
                                                        tok[:, bass.ds(s.group(8 - h), 1)], 1.0, None, ALU.mult)
                            for h in range(2):
                                nc.vector.max_index(topi[:, h, :], top[:, h, :], pr[:, h, :]).then_inc(rt["topi"], 1)
                            dve.wait_ge(rt["topi"], n * 2)
                            nc.vector.tensor_copy(topf[:], topi[:, :, 0:TOPK]).then_inc(rt["topf"], 1)
                            dve.wait_ge(rt["topf"], n)
                            for h in range(2):
                                nc.vector.tensor_tensor(hot[:, h], e_f[:].unsqueeze(1).to_broadcast([P, TOPK, E]),
                                                        bcast(topf[:, h, :], [P, TOPK, E]), ALU.is_equal
                                                        ).then_inc(rt["hot"], 1)
                            dve.wait_ge(rt["hot"], n * 2)
                            nc.vector.tensor_tensor(picked[:], hot[:, :, 0, :], hot[:, :, 1, :], ALU.add
                                                    ).then_inc(rt["picked"], 1)
                            dve.wait_ge(rt["picked"], n)
                            dve.wait_ge(rt["first"], n)
                            nc.vector.tensor_tensor(before[:, 1, :], before[:, 0, :], picked[:, 0, :], ALU.add
                                                    ).then_inc(rt["before"], 1)
                            dve.wait_ge(rt["before"], n)
                            nc.vector.tensor_tensor(counted[:], before[:, 1, :], picked[:, 1, :], ALU.add
                                                    ).then_inc(rt["counted"], 1)
                            dve.wait_ge(rt["counted"], n)
                        if (j, c) == (2, 3) and s.has(OUT):
                            s.wait(dve, r_done, OUT)
                            s.wait(dve, o_saved, OUT)
                            nc.vector.tensor_tensor(o_sb[:], ps_a[:], o_sb[:], ALU.mult).then_inc(scaled, 1)
                        if (j, c) == (3, 1) and s.has(OUT):
                            i = s.ring(OUT, 2)
                            s.wait(dve, scaled, OUT)
                            if s.has(OUT + 2):
                                dve.wait_ge(x1_st[i], s.rounds(OUT + 2, 2) * 16)
                            dve.wait_ge(res_ld[s.ring(OUT, 4)], s.rounds(OUT, 4) * 16)
                            nc.vector.tensor_tensor(x1[i][:], o_sb[:], xres[s.ring(OUT, 4)][:], ALU.add).then_inc(x1_ready, 1)
                        if (j, c) == (3, 3) and s.has(0):
                            i = s.ring(0, 2)
                            s.wait(dve, max_done, 0, each=16)
                            s.wait(dve, m_done, 2)
                            nc.vector.tensor_copy(nmax_hl[i][:, :, 0:HPG].bitcast(F32R), nmax[i][:]).then_inc(nmax_hi, 1)
                            s.wait(dve, nmax_hi, 0)
                            nc.vector.tensor_tensor(nmax_hl[i][:, :, HPG:MROWS], nmax[i][:], nmax_hl[i][:, :, 0:HPG],
                                                    ALU.subtract).then_inc(nmax_ready, 1)
                        if (j, c) == (3, 3) and s.has(OUT):
                            i = s.ring(OUT, 2)
                            s.wait(dve, x1_ready, OUT)
                            nc.vector.bn_stats(st2[i][:, 0:6], x1[i][:]).then_inc(stat2, 1)
                        if (j, c) == (3, 3) and s.k % 2 == 0 and s.has(8):
                            n = batch(8)
                            dve.wait_ge(rt["pos"], n)
                            pos = ps_b[:, 0:2 * E].rearrange("p (h e) -> p h e", h=2)
                            nc.vector.tensor_scalar(over[:], pos, float(CAP), float(1 << 20), ALU.is_ge, ALU.mult
                                                    ).then_inc(rt["over"], 1)
                            nc.vector.tensor_tensor(place[:], pos, e_row0[:].unsqueeze(1).to_broadcast([P, 2, E]), ALU.add
                                                    ).then_inc(rt["place0"], 1)
                            dve.wait_ge(rt["over"], n)
                            dve.wait_ge(rt["place0"], n)
                            nc.vector.tensor_tensor(place[:], place[:], over[:], ALU.add).then_inc(rt["place"], 1)
                            dve.wait_ge(rt["place"], n)
                            for h in range(2):
                                nc.vector.tensor_tensor(chosen[:, h], hot[:, h],
                                                        place[:, h, :].unsqueeze(1).to_broadcast([P, TOPK, E]), ALU.mult
                                                        ).then_inc(rt["chosen"], 1)
                            dve.wait_ge(rt["chosen"], n * 2)
                            nc.vector.reduce_sum(rowf[:], chosen[:], AX).then_inc(rt["rowf"], 1)
                            dve.wait_ge(rt["rowf"], n)
                            nc.vector.tensor_copy(rowd[s.ring(8, 4) // 2][:], rowf[:].rearrange("p h k -> p (h k)")
                                                  ).then_inc(rt["rowd"], 1)
                            for h in range(2):
                                last = nc.vector.tensor_tensor(xrow[s.ring(8 - h, 8)][:, GATE0:GATE0 + E], pr[:, h, :],
                                                               picked[:, h, :], ALU.mult)
                            last.then_inc(rt["gate"], 1)
            dve.wait_ge(total_done, 1)
            nc.vector.tensor_copy(totals[:], ps_a[:, 0:E]).then_inc(total_ready, 1)
            dve.wait_ge(total_ready, 1)

        @block.tensor
        def _(pe):
            pe.wait_ge(pool_const, 5)
            pe.wait_ge(sel_ready, 4)
            pe.wait_ge(const_ld, 32)
            for s in slots(pe):
                for j in range(HPG):
                    for c in range(NC4):
                        cols = slice(P * c, P * c + P)
                        if s.has(0):
                            i = s.ring(0, 4)
                            if j == 0 and c == 0:
                                pe.wait_ge(stack_ld[i], s.rounds(0, 4) * (16 * COPIES))
                            s.wait(pe, max_done, 0, each=16, minus=17 - (4 * j + c))
                            nc.tensor.matmul(ps_s[c % 2][:], qst[i][0:STACK, j, cols], kst[i][0:STACK, j, :],
                                             start=True, stop=True).then_inc(s_done, 1)
                        if s.has(ST):
                            i = s.ring(ST, 4)
                            if j == 0 and c == 0:
                                pe.wait_ge(mrow_ld[i], s.rounds(ST, 4) * 16)
                            s.wait(pe, exp_done, ST, each=16, minus=17 - (4 * j + c))
                            nc.tensor.matmul(ps_t[c % 2][:], kst[i][0:STACK + MROWS, j, cols],
                                             qst[i][0:STACK + MROWS, j, :], start=True, stop=True).then_inc(st_done, 1)
                        if c == 1 and s.has(PV):
                            if j == 0:
                                s.wait(pe, exp_done, PV, each=16)
                                s.wait(pe, vt_ready, PV)
                                s.wait(pe, o_saved, PV + 1)
                            for h in range(HPG):
                                hd = slice(HD * h, HD * h + HD)
                                nc.tensor.matmul(ps_o[hd, :], vt[s.ring(PV, 4)][:, j, hd], probs[s.ring(PV, 2)][:, h, j, :],
                                                 start=(j == 0), stop=(j == NC4 - 1))
                        if c == 3 and s.has(PV):
                            if j == 0:
                                s.wait(pe, l_saved, PV + 1)
                            for h in range(HPG):
                                hd = slice(HD * h, HD * h + HD)
                                last = nc.tensor.matmul(ps_l[hd, :], ones[:, 0:HD], probs[s.ring(PV, 2)][:, h, j, :],
                                                        start=(j == 0), stop=(j == NC4 - 1))
                            if j == NC4 - 1:
                                last.then_inc(pv_done, 1)
                        if (j, c) == (1, 1) and s.has(0):
                            if s.has(OUT):
                                s.wait(pe, linv_ready, OUT)
                            s.wait(pe, vt_ready, 1)
                            s.wait(pe, scaled, OUT + 1)
                            pe.wait_ge(c_ld[s.ring(0, 4)], s.rounds(0, 4) * 16)
                            for q in range(NC4):
                                last = nc.tensor.transpose(ps_a[:, P * q:P * q + P], ct[s.ring(0, 4)][:, P * q:P * q + P],
                                                           ident[:])
                            last.then_inc(vt_done, 1)
                        if (j, c) == (2, 1) and s.has(OUT):
                            s.wait(pe, vt_ready, 0)
                            s.wait(pe, linv_ready, OUT)
                            for q in range(NC4):
                                for h in range(HPG):
                                    last = nc.tensor.matmul(
                                        ps_a[HD * h:HD * h + HD, P * q:P * q + P],
                                        linv[s.ring(OUT, 2)][:, q, h:h + 1].to_broadcast([P, HD]),
                                        ident[:], start=True, stop=True)
                            last.then_inc(r_done, 1)
                    if j == 0 and s.has(OUT):
                        s.wait(pe, l_saved, OUT)
                        s.wait(pe, vt_ready, 1)
                        s.wait(pe, scaled, OUT + 1)
                        for c in range(NC4):
                            last = nc.tensor.transpose(ps_a[:, P * c:P * c + P], l_sb[:, P * c:P * c + P],
                                                       ident[:])
                        last.then_inc(lt_done, 1)
                    if j == 0 and s.has(1):
                        s.wait(pe, nmax_ready, 1)
                        s.wait(pe, mrow_ready, 2)
                        s.wait(pe, lg_saved, LN + 1)
                        for c in range(NC4):
                            last = nc.tensor.transpose(ps_b[0:HD, P * c:P * c + P], nmax_hl[s.ring(1, 2)][:, c, :],
                                                       ident[:])
                        last.then_inc(m_done, 1)
                    if j == 1 and s.has(LN):
                        s.wait(pe, mrow_ready, 1)
                        s.wait(pe, lg_saved, LN + 1)
                        s.wait(pe, x2_ready, LN)
                        for c in range(NC4):
                            last = nc.tensor.transpose(ps_b[:, P * c:P * c + P], xrow[s.ring(LN, 8)][:, P * c:P * c + P],
                                                       ident[:])
                        last.then_inc(x2t_done, 1)
                    if j == 2 and s.k % 2 == 0 and s.has(8):
                        n = s.it * (U // 2) + ((s.k - 8) // 2 + 1)
                        s.wait(pe, x2t_ready, LN)
                        s.wait(pe, lg_saved, LN + 1)
                        s.wait(pe, mrow_ready, 1)
                        pe.wait_ge(rt["before"], n)
                        pos = ps_b[:, 0:2 * E]
                        nc.tensor.matmul(pos, earlier[:], picked[:].rearrange("p h e -> p (h e)"), start=True, stop=False)
                        nc.tensor.matmul(pos, ones[:], before[:].rearrange("p h e -> p (h e)"), start=False, stop=True
                                         ).then_inc(rt["pos"], 1)
                    if j == 3 and s.has(LN):
                        s.wait(pe, x2t_ready, LN)
                        if s.k % 2 == 0 and s.has(8):
                            n = s.it * (U // 2) + ((s.k - 8) // 2 + 1)
                            pe.wait_ge(rt["place0"], n)
                        for c in range(NC4):
                            last = nc.tensor.matmul(ps_b[:, 0:E], x2t[:, P * c:P * c + P], wg_sb[:, c, :],
                                                    start=(c == 0), stop=(c == NC4 - 1))
                        last.then_inc(lg_done, 1)
            pe.wait_ge(rt["counted"], B)
            pe.wait_ge(scaled, G)
            nc.tensor.matmul(ps_a[:, 0:E], ones[:], counted[:], start=True, stop=True).then_inc(total_done, 1)


def experts(nc, w1, w2, out_rows, disp, totals):
    N = E * TILES
    with ExitStack() as stack:
        def sb(name, shape, dt=F32):
            return stack.enter_context(nc.sbuf_tensor(name, shape, dt))

        def sem(name):
            return stack.enter_context(nc.semaphore(name))

        ident = sb("ident2", [P, P])
        w1hi = sb("w1hi", [P, NC4, FF], F32R)
        w1lo = sb("w1lo", [P, NC4, FF], F32R)
        w2hi = sb("w2hi", [P, NF, D], F32R)
        w2lo = sb("w2lo", [P, NF, D], F32R)
        raw = [sb(f"raw{i}", [P, 2 * D]) for i in range(NRAW)]
        xin = sb("xin", [P, 2, ROW])
        xhi = sb("xhi", [P, NC4, T], F32R)
        xlo = sb("xlo", [P, NC4, T], F32R)
        hhi = sb("hhi", [P, NF, T], F32R)
        hlo = sb("hlo", [P, NF, T], F32R)
        gates = sb("gates", [P, TILES * 2 * E])
        ids = sb("ids", [P, TILES, 2], I32)
        zeros = sb("zeros2", [P, 2], I32)
        turn = [sb(f"turn{h}", [P, 1], I32) for h in range(2)]
        y = [sb(f"y{h}", [P, D]) for h in range(2)]

        ps_x = [stack.enter_context(nc.psum_tensor(f"ps_x{i}", [P, 2, T], F32)) for i in range(2)]
        ps_h = [stack.enter_context(nc.psum_tensor(f"ps_h{i}", [P, 2, T], F32)) for i in range(4)]
        ps_y = [stack.enter_context(nc.psum_tensor(f"ps_y{i}", [P, D], F32)) for i in range(2)]

        zeroed = sem("zeroed2")
        ident_ready = sem("ident_ready")
        raw_ld = [sem(f"raw_ld{i}") for i in range(NRAW)]
        xin_ld = sem("xin_ld")
        w_hi = sem("w_hi")
        w_ready = sem("w_ready")
        xt_done = sem("xt_done")
        xhi_ready = sem("xhi_ready")
        xlo_ready = sem("xlo_ready")
        gates_kept = sem("gates_kept")
        ids_kept = sem("ids_kept")
        turn_taken = sem("turn_taken")
        h_done = sem("h_done")
        hhi_ready = sem("hhi_ready")
        h_ready = sem("h_ready")
        y_done = sem("y_done")
        y_ready = sem("y_ready")
        y_added = sem("y_added")

        disp_t = disp.rearrange("(n h p) w -> n p h w", h=2, p=P)
        w1_p = w1.rearrange("e (c p) f -> e c p f", p=P)
        w2_p = w2.rearrange("e (f p) d -> e p f d", p=P)
        HALF = FF // 2

        def piece(t1, t2, i):
            if i < 8:
                return t1[:, i % NC4, HALF * (i // NC4):HALF * (i // NC4) + HALF]
            f = 2 * (i - 8)
            return t2[:, f:f + 2, :].rearrange("p f d -> p (f d)")

        def rows_of(eng, e):
            return eng.value_load(totals[0:1, bass.ds(e, 1)], min_val=0, max_val=S)

        block = stack.enter_context(nc.Block())

        @block.sync
        def _(sp):
            def weights(e, pieces, first):
                for i in pieces:
                    if not (first and i < NRAW):
                        sp.wait_ge(w_ready, e * PIECES + (i - NRAW + 1))
                    if i < 8:
                        src = w1_p[bass.ds(e, 1), i % NC4, :, HALF * (i // NC4):HALF * (i // NC4) + HALF].rearrange(
                            "e p f -> (e p) f")
                        dst = raw[i % NRAW][:]
                    else:
                        f = 2 * (i - 8)
                        src = w2_p[bass.ds(e, 1), :, f:f + 2, :].rearrange("e p f d -> (e p) f d")
                        dst = raw[i % NRAW][:].rearrange("p (f d) -> p f d", f=2)
                    sp.dma_start(dst, src).then_inc(raw_ld[i % NRAW], 16)

            def tile_in(n, first=False):
                if not first:
                    sp.wait_ge(xt_done, n * 2)
                    sp.wait_ge(gates_kept, n)
                    sp.wait_ge(ids_kept, n)
                sp.dma_start(xin[:], disp_t[bass.ds(n, 1)].rearrange("n p h w -> (n p) h w")).then_inc(xin_ld, 16)

            tile_in(0, first=True)
            weights(0, range(12), True)
            tile_in(1)
            weights(0, range(12, PIECES), True)
            with sp.Fori(1, E) as e:
                weights(e, range(NRAW), False)
                with sp.Fori(2, TILES + 1) as t:
                    tile_in((e - 1) * TILES + t)
                weights(e, range(NRAW, 12), False)
                tile_in(e * TILES + 1)
                weights(e, range(12, PIECES), False)
            with sp.Fori(2, TILES) as t:
                tile_in((E - 1) * TILES + t)

        @block.gpsimd
        def _(pool):
            nc.gpsimd.memset(zeros[:], 0).then_inc(zeroed, 1)
            nc.gpsimd.memset(ident[:], 0.0).then_inc(zeroed, 1)
            pool.wait_ge(zeroed, 2)
            nc.gpsimd.affine_select(out=ident[:], in_=ident[:], compare_op=ALU.not_equal, fill=1.0, base=0,
                                    pattern=[[-1, P]], channel_multiplier=1).then_inc(ident_ready, 1)

            def keep_ids(n, t):
                pool.wait_ge(xin_ld, n * 16 + 16)
                nc.gpsimd.tensor_tensor(ids[:, t], xin[:, :, IDCOL].bitcast(I32), zeros[:], ALU.add).then_inc(ids_kept, 1)

            def add(n, t):
                pool.wait_ge(ids_kept, n + 1)
                for h in range(2):
                    pool.wait_ge(y_ready, n * 2 + (h + 1))
                    nc.gpsimd.tensor_tensor(turn[h][:], ids[:, t, h:h + 1], zeros[:, 0:1], ALU.add).then_inc(turn_taken, 1)
                    nc.gpsimd.indirect_dma_start(
                        out=out_rows[:, :], in_=y[h][:], in_offset=None,
                        out_offset=bass.IndirectOffsetOnAxis(ap=ids[:, t, h:h + 1].bitcast(U32), axis=0),
                        bounds_check=S - 1, oob_is_err=False, compute_op=ALU.add).then_inc(y_added, 16)
                    pool.wait_ge(y_added, n * 32 + 16 * (h + 1))
                    pool.wait_ge(turn_taken, n * 2 + (h + 1))

            keep_ids(0, 0)
            with pool.Fori(0, E - 1) as e:
                for t in range(TILES):
                    keep_ids(e * TILES + (t + 1), (t + 1) % TILES)
                    add(e * TILES + t, t)
            for t in range(TILES - 1):
                keep_ids(N - TILES + t + 1, t + 1)
                add(N - TILES + t, t)
            add(N - 1, TILES - 1)

        @block.scalar
        def _(act):
            def cut(e, i):
                act.wait_ge(raw_ld[i % NRAW], e * (16 * PIECES // NRAW) + 16 * (i // NRAW + 1))
                nc.scalar.activation(piece(w1hi, w2hi, i), raw[i % NRAW][:], ACT.Copy).then_inc(w_hi, 1)

            def x_in(n):
                for i in range(2):
                    act.wait_ge(xt_done, n * 2 + (i + 1))
                    nc.scalar.activation(xhi[:, 2 * i:2 * i + 2, :], ps_x[i][:], ACT.Copy).then_inc(xhi_ready, 1)

            def tile(n, e=None, free=True):
                for f in range(NF // 2):
                    act.wait_ge(h_done, n * 8 + (f + 1))
                    nc.scalar.activation(hhi[:, 2 * f:2 * f + 2, :], ps_h[f % 4][:], ACT.Relu).then_inc(hhi_ready, 1)
                    if e is not None:
                        if free and f == 0:
                            act.wait_ge(y_done, n * 2)
                        cut(e, 8 + f)

            def later_tiles(e):
                rows = rows_of(act, e)
                with act.Fori(1, TILES) as t:
                    n = e * TILES + t
                    x_in(n)
                    with act.If(rows > t * T):
                        tile(n)
                    with act.Else():
                        act.wait_ge(hhi_ready, n * 8)
                        act.sem_inc(hhi_ready, 8)

            x_in(0)
            for i in range(8):
                cut(0, i)
            tile(0, 0, free=False)
            later_tiles(0)
            with act.Fori(1, E) as e:
                for i in range(4):
                    cut(e, i)
                x_in(e * TILES)
                for i in range(4, 8):
                    cut(e, i)
                tile(e * TILES, e)
                later_tiles(e)

        @block.vector
        def _(dve):
            def cut(e, i):
                dve.wait_ge(w_hi, e * PIECES + (i + 1))
                nc.vector.tensor_tensor(piece(w1lo, w2lo, i), raw[i % NRAW][:], piece(w1hi, w2hi, i).bitcast(F32),
                                        ALU.subtract).then_inc(w_ready, 1)

            def x_in(n):
                for i in range(2):
                    dve.wait_ge(xhi_ready, n * 2 + (i + 1))
                    nc.vector.tensor_tensor(xlo[:, 2 * i:2 * i + 2, :], ps_x[i][:],
                                            xhi[:, 2 * i:2 * i + 2, :].bitcast(F32), ALU.subtract).then_inc(xlo_ready, 1)

            def y_half(n, e, t, h):
                dve.wait_ge(y_done, n * 2 + (h + 1))
                dve.wait_ge(gates_kept, n + 1)
                nc.vector.tensor_scalar(y[h][:], ps_y[h][:], gates[:, bass.ds(t * (2 * E) + e + E * h, 1)], None, ALU.mult
                                        ).then_inc(y_ready, 1)

            def y_out_whole(n, e, t, free=True):
                for h in range(2):
                    if free:
                        dve.wait_ge(y_added, n * 32 + (16 * h - 16))
                    y_half(n, e, t, h)

            def y_out(n, e, t, rows):
                for h in range(2):
                    with dve.If(rows > t * T + P * h):
                        dve.wait_ge(y_added, n * 32 + (16 * h - 16))
                        y_half(n, e, t, h)
                    with dve.Else():
                        dve.wait_ge(y_ready, n * 2 + h)
                        dve.sem_inc(y_ready, 1)

            def keep_gates(n, t):
                dve.wait_ge(xin_ld, n * 16 + 16)
                nc.vector.tensor_copy(gates[:, bass.ds(t * (2 * E), 2 * E)].rearrange("p (h e) -> p h e", h=2),
                                      xin[:, :, GATE0:GATE0 + E]).then_inc(gates_kept, 1)

            def h_low(n, e=None):
                for f in range(NF // 2):
                    dve.wait_ge(hhi_ready, n * 8 + (f + 1))
                    nc.vector.scalar_tensor_tensor(hlo[:, 2 * f:2 * f + 2, :], ps_h[f % 4][:], 0.0,
                                                   hhi[:, 2 * f:2 * f + 2, :].bitcast(F32), ALU.max, ALU.subtract
                                                   ).then_inc(h_ready, 1)
                    if e is not None:
                        cut(e, 8 + f)

            def later_h_low(n, t, rows):
                with dve.If(rows > t * T):
                    h_low(n)
                with dve.Else():
                    dve.wait_ge(h_ready, n * 8)
                    dve.sem_inc(h_ready, 8)

            def later_tiles(e, first=False, last=False):
                rows = rows_of(dve, e)
                x_in(e * TILES + 1)
                keep_gates(e * TILES + 1, 1)
                y_out_whole(e * TILES, e, 0, free=not first)
                later_h_low(e * TILES + 1, 1, rows)
                with dve.Fori(2, TILES - 1) as t:
                    n = e * TILES + t
                    x_in(n)
                    keep_gates(n, t)
                    y_out(n - 1, e, t - 1, rows)
                    later_h_low(n, t, rows)
                t, n = TILES - 1, e * TILES + (TILES - 1)
                x_in(n)
                keep_gates(n, t)
                with dve.If(rows > t * T):
                    y_out_whole(n - 1, e, t - 1)
                    h_low(n)
                with dve.Else():
                    if not last:
                        for i in range(4):
                            cut(e + 1, i)
                    y_out(n - 1, e, t - 1, rows)
                    dve.wait_ge(h_ready, n * 8)
                    dve.sem_inc(h_ready, 8)

            def first_tile(e):
                rows_before = rows_of(dve, e - 1)
                with dve.If(rows_before > (TILES - 1) * T):
                    for i in range(4):
                        cut(e, i)
                x_in(e * TILES)
                keep_gates(e * TILES, 0)
                for i in range(4, 8):
                    cut(e, i)
                y_out(e * TILES - 1, e - 1, TILES - 1, rows_before)
                h_low(e * TILES, e)

            x_in(0)
            for i in range(8):
                cut(0, i)
            keep_gates(0, 0)
            h_low(0, 0)
            later_tiles(0, first=True)
            with dve.Fori(1, E - 1) as e:
                first_tile(e)
                later_tiles(e)
            first_tile(E - 1)
            later_tiles(E - 1, last=True)
            y_out(N - 1, E - 1, TILES - 1, rows_of(dve, E - 1))

        @block.tensor
        def _(pe):
            pe.wait_ge(ident_ready, 1)

            def x_in(n, first=False):
                pe.wait_ge(xin_ld, n * 16 + 16)
                if not first:
                    pe.wait_ge(xlo_ready, n * 2)
                for i in range(2):
                    for c in range(2):
                        for h in range(2):
                            k = 2 * i + c
                            last = nc.tensor.transpose(ps_x[i][:, c, P * h:P * h + P], xin[:, h, P * k:P * k + P], ident[:])
                    last.then_inc(xt_done, 1)

            def up(n, e=None, first=False):
                pe.wait_ge(xlo_ready, n * 2 + 2)
                for f in range(NF):
                    if e is not None and f % 8 == 0:
                        pe.wait_ge(w_ready, e * PIECES + (NC4 * (f // 8) + NC4))
                    if f % 2 == 0 and not (first and f < 8):
                        pe.wait_ge(h_ready, n * 8 + (f // 2 - 3))
                    fs = slice(P * f, P * f + P)
                    to = ps_h[f // 2 % 4][:, f % 2, :]
                    for c in range(NC4):
                        nc.tensor.matmul(to, w1hi[:, c, fs], xhi[:, c, :], start=(c == 0), stop=False)
                        nc.tensor.matmul(to, w1hi[:, c, fs], xlo[:, c, :], start=False, stop=False)
                        last = nc.tensor.matmul(to, w1lo[:, c, fs], xhi[:, c, :], start=False, stop=(c == NC4 - 1))
                    if f % 2:
                        last.then_inc(h_done, 1)

            def down(n, h, e=None, first=False):
                if not first:
                    pe.wait_ge(y_ready, n * 2 + (h - 1))
                hs = slice(P * h, P * h + P)
                for f in range(NF):
                    if h == 0 and f % 2 == 0:
                        pe.wait_ge(h_ready, n * 8 + (f // 2 + 1))
                        if e is not None:
                            pe.wait_ge(w_ready, e * PIECES + (8 + f // 2 + 1))
                    nc.tensor.matmul(ps_y[h][:], hhi[:, f, hs], w2hi[:, f, :], start=(f == 0), stop=False)
                    nc.tensor.matmul(ps_y[h][:], hhi[:, f, hs], w2lo[:, f, :], start=False, stop=False)
                    last = nc.tensor.matmul(ps_y[h][:], hlo[:, f, hs], w2hi[:, f, :], start=False, stop=(f == NF - 1))
                last.then_inc(y_done, 1)

            def later_tile(e, t, rows, next_in=True):
                n = e * TILES + t
                with pe.If(rows > t * T):
                    up(n)
                with pe.Else():
                    pe.wait_ge(h_done, n * 8)
                    pe.sem_inc(h_done, 8)
                if next_in:
                    x_in(n + 1)
                for h in range(2):
                    with pe.If(rows > t * T + P * h):
                        down(n, h)
                    with pe.Else():
                        pe.wait_ge(y_done, n * 2 + h)
                        pe.sem_inc(y_done, 1)

            x_in(0, first=True)
            up(0, 0, first=True)
            x_in(1)
            down(0, 0, 0, first=True)
            down(0, 1, 0, first=True)
            rows0 = rows_of(pe, 0)
            with pe.Fori(1, TILES) as t:
                later_tile(0, t, rows0)
            with pe.Fori(1, E - 1) as e:
                rows = rows_of(pe, e)
                up(e * TILES, e)
                x_in(e * TILES + 1)
                down(e * TILES, 0, e)
                down(e * TILES, 1, e)
                with pe.Fori(1, TILES) as t:
                    later_tile(e, t, rows)
            up(N - TILES, E - 1)
            x_in(N - TILES + 1)
            down(N - TILES, 0, E - 1)
            down(N - TILES, 1, E - 1)
            rows7 = rows_of(pe, E - 1)
            with pe.Fori(1, TILES - 1) as t:
                later_tile(E - 1, t, rows7)
            later_tile(E - 1, TILES - 1, rows7, next_in=False)


_INS = ["x", "ctx_2048", "itok_B_779_1933", "L0_ffn_Wg", "L0_ffn_w1", "L0_ffn_w2"]


def kernel(**inputs):
    import concourse.bacc as bacc
    from concourse.bass_utils import run_bass_kernel_spmd

    nc = bacc.Bacc("TRN2", target_bir_lowering=False, num_devices=1, dynamic_dma_scratch_size=8192)
    arrays, args = {}, []
    for name in _INS:
        a = np.ascontiguousarray(inputs[name])
        arrays[f"in_{name}"] = a
        args.append(nc.dram_tensor(f"in_{name}", a.shape, mybir.dt.from_np(a.dtype), kind="ExternalInput").ap())
    out = nc.dram_tensor("out_x", (B, CH, D), F32, kind="ExternalOutput").ap()
    disp = nc.dram_tensor("dispatched", (E * CAP, ROW), F32, kind="Internal").ap()
    layer(nc, *args, out, disp)
    r = run_bass_kernel_spmd(nc, [arrays], core_ids=[0])
    return r.results[0]["out_x"]
```
